# Optimizing a Trainium2 kernel written in Bass

```python
import numpy as np
import jax
import jax.numpy as jnp

def _softmax(x, axis=-1):
    return jax.nn.softmax(x, axis=axis)

def _gelu(x):
    return jax.nn.gelu(x, approximate=True)

def _silu(x):
    return jax.nn.silu(x)

def _sigmoid(x):
    return jax.nn.sigmoid(x)

def _layernorm(x, axis=-1, eps=1e-05):
    m = jnp.mean(x, axis=axis, keepdims=True)
    v = jnp.var(x, axis=axis, keepdims=True)
    return (x - m) / jnp.sqrt(v + eps)

def _scatter_add(tgt, idx, src, axis=0):
    return tgt.at[idx].add(src)

def _segment_sum(src, seg, n):
    return jax.ops.segment_sum(src, seg, n)
kernel_name = 'mk_gnn_preln_d4_gnn_r8_87cd6f'

def setup_inputs(seed: int=0):
    np.random.seed(seed)
    _w = jnp.asarray

    def _rec_inputs():
        import jax
        import jax.numpy as jnp
        _gk = jax.random.key(seed)
        x = -0.0005121 + 1.001 * jax.random.normal(jax.random.fold_in(_gk, 1), (12500, 32), jnp.float32)
        src = jax.random.randint(jax.random.fold_in(_gk, 2), (200000,), 0, 12500, jnp.int32)
        dst = jnp.minimum((12500 * jax.random.uniform(jax.random.fold_in(_gk, 3), (200000,)) ** 2.0).astype(jnp.int32), 99999)
        _o = jnp.argsort(dst, stable=True)
        src = src[_o]
        dst = dst[_o]
        edge_attr_32 = -9.77346e-05 + 0.999888 * jax.random.normal(jax.random.fold_in(_gk, 12), (200000, 32), jnp.float32)
        edge_type_86 = jax.random.randint(jax.random.fold_in(_gk, 14), (200000,), 0, 86, jnp.int32)
        edge_weight = jax.random.uniform(jax.random.fold_in(_gk, 15), (200000,), jnp.float32, 0.0, 0.999999)
        return (x, src, dst, edge_attr_32, edge_type_86, edge_weight)
    x, src, dst, edge_attr_32, edge_type_86, edge_weight = _rec_inputs()

    def _L0_gnn_setup():
        import jax, jax.numpy as jnp
        import numpy as np
        N_NODES = 12500
        N_EDGES = 200000
        D = 32
        key = jax.random.key(seed)
        k1, k2, k3, k4, k5 = jax.random.split(key, 5)
        node_inputs = jax.random.normal(k1, (N_NODES, D), dtype=jnp.float32)
        edge_inputs = jax.random.normal(k2, (N_EDGES, D), dtype=jnp.float32)
        src = jax.random.randint(k3, (N_EDGES,), 0, N_NODES, dtype=jnp.int32)
        dst = jax.random.randint(k4, (N_EDGES,), 0, N_NODES, dtype=jnp.int32)
        lim = 1.0 / np.sqrt(D)
        W = jax.random.uniform(k5, (D, D), minval=-lim, maxval=lim, dtype=jnp.float32)
        b = jnp.zeros((D,), dtype=jnp.float32)
        eps = jnp.zeros((1,), dtype=jnp.float32)
        return {'node_inputs': node_inputs, 'edge_inputs': edge_inputs, 'src': src, 'dst': dst, 'W': W, 'b': b, 'eps': eps}
    _L0_gnn_all = _L0_gnn_setup()
    _L0_gnn_in = {k: v for k, v in _L0_gnn_all.items() if k in ('W', 'b', 'eps')}
    del _L0_gnn_all

    def _L1_gnn_setup():
        import jax, jax.numpy as jnp
        import numpy as np
        N_NODES = 6250
        N_EDGES = 100000
        INP_DIM = 32
        OUT_DIM = 32
        ATTN_DIM = 32
        NUM_RELS = 86
        NUM_BASES = 16
        GAMMA = 0.0
        key = jax.random.key(seed)
        ks = jax.random.split(key, 12)
        return {'h': jax.random.normal(ks[0], (N_NODES, INP_DIM), jnp.float32), 'weight': jax.random.normal(ks[1], (NUM_BASES, INP_DIM, OUT_DIM), jnp.float32), 'w_comp': jax.random.normal(ks[2], (NUM_RELS, NUM_BASES), jnp.float32), 'self_loop_weight': jax.random.normal(ks[3], (INP_DIM, OUT_DIM), jnp.float32), 'A1_w': jax.random.normal(ks[4], (ATTN_DIM, INP_DIM), jnp.float32), 'A1_b': jax.random.normal(ks[5], (ATTN_DIM,), jnp.float32), 'A2_w': jax.random.normal(ks[6], (ATTN_DIM, INP_DIM), jnp.float32), 'A2_b': jax.random.normal(ks[7], (ATTN_DIM,), jnp.float32), 'rel_emb': jax.random.normal(ks[8], (NUM_RELS, ATTN_DIM), jnp.float32), 'src': jax.random.randint(ks[9], (N_EDGES,), 0, N_NODES, jnp.int32), 'dst': jax.random.randint(ks[10], (N_EDGES,), 0, N_NODES, jnp.int32), 'etype': jax.random.randint(ks[11], (N_EDGES,), 0, NUM_RELS, jnp.int32)}
    _L1_gnn_all = _L1_gnn_setup()
    _L1_gnn_in = {k: v for k, v in _L1_gnn_all.items() if k in ('weight', 'w_comp', 'self_loop_weight', 'A1_w', 'A1_b', 'A2_w', 'A2_b', 'rel_emb')}
    del _L1_gnn_all

    def _L2_gnn_setup():
        import jax, jax.numpy as jnp
        import numpy as np
        N = 6250
        E = 200000
        F_IN = 32
        F_OUT = 32
        key = jax.random.key(seed)
        k_x, k_ei, k_norm, k_w, k_b = jax.random.split(key, 5)
        x = jax.random.normal(k_x, (N, F_IN), dtype=jnp.float32)
        edge_index = jax.random.randint(k_ei, (2, E), 0, N, dtype=jnp.int64)
        norm = jax.random.uniform(k_norm, (E,), dtype=jnp.float32)
        W = jax.random.normal(k_w, (F_IN, F_OUT), dtype=jnp.float32) / np.sqrt(F_IN)
        b = jax.random.normal(k_b, (F_OUT,), dtype=jnp.float32) * 0.01
        return {'x': x, 'edge_index': edge_index, 'norm': norm, 'W': W, 'b': b}
    _L2_gnn_all = _L2_gnn_setup()
    _L2_gnn_in = {k: v for k, v in _L2_gnn_all.items() if k in ('W', 'b')}
    del _L2_gnn_all

    def _L3_gnn_setup():
        import jax, jax.numpy as jnp
        import numpy as np
        N_NODES = 12500
        N_EDGES = 200000
        IN_FEAT = 32
        OUT_FEAT = 32
        key = jax.random.key(seed)
        k1, k2, k3, k4 = jax.random.split(key, 4)
        feat = jnp.ones((N_NODES, IN_FEAT), dtype=jnp.float32)
        src = jax.random.randint(k1, (N_EDGES,), 0, N_NODES, dtype=jnp.int64)
        dst = jax.random.randint(k2, (N_EDGES,), 0, N_NODES, dtype=jnp.int64)
        W = jax.random.normal(k3, (OUT_FEAT, IN_FEAT), dtype=jnp.float32) * 0.05
        b = jax.random.normal(k4, (OUT_FEAT,), dtype=jnp.float32) * 0.05
        return {'feat': feat, 'src': src, 'dst': dst, 'W': W, 'b': b}
    _L3_gnn_all = _L3_gnn_setup()
    _L3_gnn_in = {k: v for k, v in _L3_gnn_all.items() if k in ('W', 'b')}
    del _L3_gnn_all
    return {'x': x, 'src': src, 'dst': dst, 'edge_attr_32': edge_attr_32, 'edge_type_86': edge_type_86, 'edge_weight': edge_weight, 'L0_gnn_W': _L0_gnn_in['W'], 'L0_gnn_b': _L0_gnn_in['b'], 'L0_gnn_eps': _L0_gnn_in['eps'], 'L1_gnn_weight': _L1_gnn_in['weight'], 'L1_gnn_w_comp': _L1_gnn_in['w_comp'], 'L1_gnn_self_loop_weight': _L1_gnn_in['self_loop_weight'], 'L1_gnn_A1_w': _L1_gnn_in['A1_w'], 'L1_gnn_A1_b': _L1_gnn_in['A1_b'], 'L1_gnn_A2_w': _L1_gnn_in['A2_w'], 'L1_gnn_A2_b': _L1_gnn_in['A2_b'], 'L1_gnn_rel_emb': _L1_gnn_in['rel_emb'], 'L2_gnn_W': _L2_gnn_in['W'], 'L2_gnn_b': _L2_gnn_in['b'], 'L3_gnn_W': _L3_gnn_in['W'], 'L3_gnn_b': _L3_gnn_in['b']}

def reference(x, src, dst, edge_attr_32, edge_type_86, edge_weight, L0_gnn_W, L0_gnn_b, L0_gnn_eps, L1_gnn_weight, L1_gnn_w_comp, L1_gnn_self_loop_weight, L1_gnn_A1_w, L1_gnn_A1_b, L1_gnn_A2_w, L1_gnn_A2_b, L1_gnn_rel_emb, L2_gnn_W, L2_gnn_b, L3_gnn_W, L3_gnn_b):
    import jax
    import jax.numpy as jnp

    def _L0_gnn_ref(node_inputs, edge_inputs, src, dst, W, b, eps):
        import jax, jax.numpy as jnp
        import numpy as np
        N_NODES = 12500
        N_EDGES = 200000
        D = 32
        msg = jax.nn.relu(node_inputs[src] + edge_inputs)
        agg = jax.ops.segment_sum(msg, dst, num_segments=N_NODES)
        h = (1.0 + eps[0]) * node_inputs + agg
        return h @ W.T + b

    def _L1_gnn_ref(h, weight, w_comp, self_loop_weight, A1_w, A1_b, A2_w, A2_b, rel_emb, src, dst, etype):
        import jax, jax.numpy as jnp
        import numpy as np
        N_NODES = 6250
        N_EDGES = 100000
        INP_DIM = 32
        OUT_DIM = 32
        ATTN_DIM = 32
        NUM_RELS = 86
        NUM_BASES = 16
        GAMMA = 0.0
        E = src.shape[0]
        N = h.shape[0]
        x = h[src]
        y = h[dst]
        c = w_comp[etype]
        xb = jnp.einsum('ei,bio->ebo', x, weight)
        msg = jnp.einsum('eb,ebo->eo', c, xb)
        x_hat = x @ A1_w.T + A1_b
        y_hat = y @ A2_w.T + A2_b + rel_emb[etype]
        scale = jnp.sqrt(jnp.asarray(INP_DIM, h.dtype))
        a = jnp.tanh(jax.nn.relu(jnp.sum(x_hat * y_hat, axis=-1) / scale))
        a = jnp.where(a > GAMMA, a, jnp.zeros_like(a))
        nei = jax.ops.segment_sum(a[:, None] * msg, dst, num_segments=N)
        last_e = jax.ops.segment_max(jnp.arange(E, dtype=jnp.int32), dst, num_segments=N)
        last_e = jnp.clip(last_e, 0, E - 1)
        curr = h[src[last_e]] @ self_loop_weight
        in_deg = jax.ops.segment_sum(jnp.ones((E,), h.dtype), dst, num_segments=N)
        h_new = jnp.where((in_deg > 0)[:, None], nei + curr, jnp.zeros_like(nei))
        return jax.nn.relu(h_new)

    def _L2_gnn_ref(x, edge_index, norm, W, b):
        import jax, jax.numpy as jnp
        import numpy as np
        N = 6250
        E = 200000
        F_IN = 32
        F_OUT = 32
        x_j = x[edge_index[0]]
        msg = norm[:, None] * x_j
        agg = jax.ops.segment_sum(msg, edge_index[1], num_segments=x.shape[0])
        return jax.nn.relu(agg @ W + b)

    def _L3_gnn_ref(feat, src, dst, W, b):
        import jax, jax.numpy as jnp
        import numpy as np
        N_NODES = 12500
        N_EDGES = 200000
        IN_FEAT = 32
        OUT_FEAT = 32
        msgs = feat[src]
        h_N = jax.ops.segment_sum(msgs, dst, num_segments=feat.shape[0])
        return jnp.einsum('nf,of->no', h_N, W) + b
    edge_index = jnp.stack([src, dst])
    h = jnp.maximum(_layernorm(x, axis=-1), 0.0)
    x = x + _L0_gnn_ref(h, edge_attr_32, src, dst, L0_gnn_W, L0_gnn_b, L0_gnn_eps)
    h = jnp.maximum(_layernorm(x, axis=-1), 0.0)
    x = x + _L1_gnn_ref(h, L1_gnn_weight, L1_gnn_w_comp, L1_gnn_self_loop_weight, L1_gnn_A1_w, L1_gnn_A1_b, L1_gnn_A2_w, L1_gnn_A2_b, L1_gnn_rel_emb, src, dst, edge_type_86)
    h = jnp.maximum(_layernorm(x, axis=-1), 0.0)
    x = x + _L2_gnn_ref(h, edge_index, edge_weight, L2_gnn_W, L2_gnn_b)
    h = jnp.maximum(_layernorm(x, axis=-1), 0.0)
    x = x + _L3_gnn_ref(h, src, dst, L3_gnn_W, L3_gnn_b)
    return x

_drawn_inputs = setup_inputs


def setup_inputs(seed=0):
    import zlib

    import numpy as np

    out = dict(_drawn_inputs(seed))
    spreads = {'L0_gnn_b': (0.0, 0.1)}
    factors = {'edge_weight': 4.898, 'L2_gnn_b': 200.0, 'L3_gnn_b': 56.022}
    for name, (base, spread) in spreads.items():
        noise = np.random.default_rng([zlib.crc32(name.encode()), seed]).standard_normal(out[name].shape)
        drawn = base * np.exp(spread * noise) if base else spread * noise
        out[name] = jnp.asarray(drawn.astype(out[name].dtype))
    for name, factor in factors.items():
        out[name] = (out[name] * factor).astype(out[name].dtype)
    return out
```

```python
import concourse.bass as bass
from concourse import mybir
from contextlib import ExitStack

F32 = mybir.dt.float32
I32 = mybir.dt.int32
BF16 = mybir.dt.bfloat16
ALU = mybir.AluOpType
ACT = mybir.ActivationFunctionType
AX = mybir.AxisListType

P = 128
N_NODES, N_EDGES, D = 12500, 200000, 32
RELS, BASES = 86, 16
EPS = 1e-5

BLOCKS = -(-N_NODES // P)
LAST_NODES = N_NODES - (BLOCKS - 1) * P
TILES = -(-N_EDGES // P)
ROWCH = -(-TILES // P)
FULL_CH = TILES // P
TAIL_TILES = N_EDGES // P - FULL_CH * P
HALF = N_EDGES - (N_EDGES // P) * P
EXTRAS = BLOCKS - 1
BODY, HB = 8, 4
STEPS = -(-(TILES + EXTRAS) // BODY) * BODY
C = STEPS // BODY
LOOK = HB
MAIN = (N_EDGES // P) // BODY
TAIL = STEPS - MAIN * BODY
FAR = float(1 << 20)
FEAT = BLOCKS * D
BANK = 512
GROUPS = -(-BLOCKS // 4)
BANKS = -(-FEAT // BANK)
BAS1 = BASES + 1
MSG = D * BAS1
ROW1 = MSG + D
YC = BASES + D


def gnn(nc, x_in, src, dst, edge_attr, etype, weight, W0, b0, eps0, W1, wcomp, wself, A1, A1b, A2, A2b,
        relemb, W2, b2, W3, b3, out):
    tableD = [nc.dram_tensor(f"table{l}", (BLOCKS * P, ROW1 if l == 1 else D), F32, kind="Internal").ap()
              for l in range(4)]
    rowsD = nc.dram_tensor("edge_rows", (ROWCH * P, 5 * P), F32, kind="Internal").ap()
    stepsD = nc.dram_tensor("step_rows", (STEPS + LOOK, 2 * P), BF16, kind="Internal").ap()
    windowD = nc.dram_tensor("step_window", (STEPS + LOOK, 1), I32, kind="Internal").ap()
    attrD = nc.dram_tensor("attr_tail", (TAIL * P, D), F32, kind="Internal").ap()

    ctx = ExitStack()
    with ctx:
        ctx.enter_context(nc.allow_non_contiguous_dma("small weights and window offsets"))

        def sb(name, shape, dt=F32):
            return ctx.enter_context(nc.sbuf_tensor(name, shape, dt))

        def sem(name):
            return ctx.enter_context(nc.semaphore(name))

        def pair(name):
            return [sem(f"{name}_{h}") for h in range(2)]

        x = sb("x", [P, BLOCKS, D])
        h = sb("h", [P, BLOCKS, D])
        t = sb("t", [P, BLOCKS, D])
        tT = sb("tT", [P, GROUPS * P])
        tabs = sb("tabs", [P, 4, STEPS])
        DLOC, SRC, WGT, LAST, ETY = range(5)
        srcT = sb("srcT", [P, STEPS + BODY], I32)
        window = sb("window", [1, STEPS + LOOK], I32)
        onehot = sb("onehot", [P, 2, HB, P])
        msg = sb("msg", [P, 2, HB, D])
        attr = sb("attr", [P, 2, HB, D])
        grow = sb("grow", [P, 2, HB, D])
        total = sb("total", [P, 2, HB, D])
        idx = sb("idx", [P, 2, HB], I32)
        iota_i = sb("iota_i", [P, P], I32)
        iota = sb("iota", [P, P])
        part_i = sb("part_i", [P, 1], I32)
        part = sb("part", [P, 1])
        part1 = sb("part1", [P, 1])
        thr = sb("thr", [P, EXTRAS])
        ident = sb("ident", [P, P])
        zeros = sb("zeros", [1, BANK])
        ones = sb("ones", [P, P])
        nat = sb("nat", [P, 2, P])
        wdiag = sb("wdiag", [P, 3, P])
        anat = sb("anat", [D, 2, 4, D])
        wq = sb("wq", [P, MSG + 2 * D])
        biasrow = sb("biasrow", [1, 3, BANK])
        bias1 = sb("bias1", [P, MSG // 2 + 2 * D])
        relc = sb("relc", [P, YC])
        opeps = sb("opeps", [P, 1])
        small = sb("small", [P, 6, BLOCKS])
        arena = sb("arena", [P, 19600])

        used = [0]

        def region(n, dt=F32):
            a = arena[:, used[0]:used[0] + n]
            used[0] += n
            return a if dt == F32 else a.bitcast(dt)

        raw = region(4 * ROWCH * P, I32).rearrange("p (a c e) -> p a c e", a=4, c=ROWCH)
        rows = region(ROWCH * 5 * P).rearrange("p (c a e) -> p c a e", c=ROWCH, a=5)
        rloc = region(ROWCH * P).rearrange("p (c e) -> p c e", c=ROWCH)
        rbf = region(ROWCH * P, BF16).rearrange("p (c a e) -> p c a e", c=ROWCH, a=2)
        xrow = region(5 * P).rearrange("p (a e) -> p a e", a=5)
        xattr = arena[:, 0:P * D]
        xloc = region(P)
        xbf = region(P, BF16).rearrange("p (a e) -> p a e", a=2)
        padbf = region(P, BF16)
        tcol = region(16)
        tcoli = region(16, I32)
        firstw = region(2 * ROWCH).rearrange("p (a c) -> p a c", a=2)
        firstwi = region(2 * ROWCH, I32).rearrange("p (a c) -> p a c", a=2)
        before = tT[:, 0:ROWCH * EXTRAS].rearrange("p (c w) -> p c w", c=ROWCH)
        wnat = tT[:, ROWCH * EXTRAS:ROWCH * EXTRAS + BAS1 * D].rearrange("p (b o) -> p b o", b=BAS1)
        used[0] = 0
        g1 = region(2 * HB * ROW1).rearrange("p (h u f) -> p h u f", h=2, u=HB)
        prod = region(HB * MSG).rearrange("p (u o b) -> p u o b", u=HB, o=D)
        rowb = region(2 * HB * P, BF16).rearrange("p (h u a e) -> p h u a e", h=2, u=HB, a=2)
        nodeT = region(2 * HB * P).rearrange("p (h u e) -> p h u e", h=2, u=HB)
        relT = region(2 * HB * P).rearrange("p (h u e) -> p h u e", h=2, u=HB)
        yc = region(2 * HB * YC).rearrange("p (h u f) -> p h u f", h=2, u=HB)
        yprod = region(HB * D).rearrange("p (u f) -> p u f", u=HB)
        coef = region(HB * BAS1).rearrange("p (u b) -> p u b", u=HB)
        score = region(2 * HB).rearrange("p (h u) -> p h u", h=2)
        pos = region(2 * HB).rearrange("p (h u) -> p h u", h=2)
        att = region(2 * HB).rearrange("p (h u) -> p h u", h=2)
        trow = region(4 * ROW1).rearrange("p (r f) -> p r f", r=4)
        y = t

        ps = ctx.enter_context(nc.psum_tensor("ps", [P, 8 * BANK], F32))
        acc = ps[:, 0:FEAT]
        ps7 = ps[:, 7 * BANK:7 * BANK + HB * YC].rearrange("p (u f) -> p u f", u=HB)

        loaded = sem("inputs_loaded")
        edges_loaded = sem("edges_loaded")
        pads_set = sem("pads_set")
        consts = sem("consts_ready")
        ident_ready = sem("identity_ready")
        dve_chain = sem("dve_chain")
        act_chain = sem("act_chain")
        wts_T = sem("weights_transposed")
        wts_ready = sem("weights_ready")
        rows_ready = sem("rows_ready")
        rows_out = sem("rows_written")
        before_ready = sem("before_ready")
        count_done = sem("extra_tiles_counted")
        extra_ready = sem("extra_tiles_ready")
        extra_rows = sem("extra_rows_gathered")
        extra_attr = sem("extra_attr_gathered")
        local_ready = sem("local_nodes_ready")
        xlocal_ready = sem("extra_local_ready")
        tabs_T = sem("tables_transposed")
        tabs_copied = sem("tables_copied")
        tabs_ready = sem("tables_ready")
        steps_out = sem("steps_written")
        window_loaded = sem("window_loaded")
        tail_ready = sem("attr_tail_written")
        var_ready = sem("variance_ready")
        std_ready = sem("std_ready")
        h_ready = sem("h_ready")
        table_out = [sem(f"table_written_{l}") for l in range(4)]
        hT_done = sem("transposed")
        hT_copied = sem("transposes_copied")
        lin_done = sem("linear_done")
        t_ready = sem("t_ready")
        acc_free = sem("sums_read")
        idx_ready = pair("idx_ready")
        gathered = [pair(f"gathered{l}") for l in range(4)]
        row_used = pair("gathered_used")
        attr_loaded = pair("attr_loaded")
        summed = sem("edge_sum_ready")
        msg_ready = pair("msg_ready")
        mm_done = pair("scatter_done")
        p1_done = sem("node_products_done")
        p1_copied = sem("node_products_copied")
        p1_biased = sem("node_products_copied_by_vector")
        p1_out = pair("node_products_written")
        steps_loaded = pair("step_rows_loaded")
        sel_ready = pair("selectors_ready")
        yc_done = pair("yc_done")
        yc_copied = sem("yc_copied")
        yprod_ready = sem("yprod_ready")
        score_ready = pair("score_ready")
        pos_ready = sem("positive_score_ready")
        att_ready = pair("attention_ready")
        coef_ready = pair("coef_ready")
        stored = sem("output_stored")

        block = ctx.enter_context(nc.Block())

        @block.sync
        def _(sp):
            n_full = FULL_CH * P * P
            n_tail = n_full + TAIL_TILES * P
            sp.wait_ge(pads_set, 4)

            def edge_rows(to, of, shift):
                sp.dma_start(to[:, 0:FULL_CH, :], of[shift:n_full + shift].rearrange("(c p e) -> p c e", p=P, e=P)
                             ).then_inc(edges_loaded, 16)
                sp.dma_start(to[0:TAIL_TILES, FULL_CH, :],
                             of[n_full + shift:n_tail + shift].rearrange("(p e) -> p e", e=P)
                             ).then_inc(edges_loaded, 16)
                sp.dma_start(to[TAIL_TILES:TAIL_TILES + 1, FULL_CH, 0:HALF - shift],
                             of[n_tail + shift:N_EDGES].rearrange("(a e) -> a e", a=1)).then_inc(edges_loaded, 16)

            edge_rows(raw[:, 0], dst, 0)
            edge_rows(raw[:, 1], dst, 1)
            edge_rows(raw[:, 2], src, 0)
            edge_rows(raw[:, 3], etype, 0)
            edge_rows(rows[:, :, WGT, :], weight, 0)
            sp.dma_start(attrD[0:N_EDGES - MAIN * BODY * P, :], edge_attr[MAIN * BODY * P:N_EDGES, :]
                         ).then_inc(tail_ready, 16)
            at = N_EDGES - MAIN * BODY * P
            sp.dma_start(attrD[at:at + P - HALF, :], edge_attr[0:P - HALF, :]).then_inc(tail_ready, 16)
            x0 = at + P - HALF
            x1 = x0 + EXTRAS * P
            sp.dma_start(attrD[x1:TAIL * P, :], edge_attr[0:TAIL * P - x1, :]).then_inc(tail_ready, 16)

            sp.wait_ge(rows_ready, 1)
            sp.dma_start(rowsD.rearrange("(c p) f -> p c f", p=P), rows[:, :, :, :].rearrange("p c a e -> p c (a e)")
                         ).then_inc(rows_out, 16)
            sp.wait_ge(local_ready, 1)
            st = stepsD.rearrange("s (a e) -> s a e", a=2)
            sp.dma_start(st[0:FULL_CH * P].rearrange("(c p) a e -> p c a e", p=P), rbf[:, 0:FULL_CH]
                         ).then_inc(steps_out, 16)
            sp.dma_start(st[FULL_CH * P:TILES], rbf[0:TILES - FULL_CH * P, FULL_CH]).then_inc(steps_out, 16)
            sp.dma_start(windowD[0:FULL_CH * P].rearrange("(c p) a -> p (c a)", p=P), firstwi[:, 1, 0:FULL_CH]
                         ).then_inc(steps_out, 16)
            sp.dma_start(windowD[FULL_CH * P:TILES], firstwi[0:TILES - FULL_CH * P, 1, FULL_CH:ROWCH]
                         ).then_inc(steps_out, 16)
            sp.wait_ge(xlocal_ready, 1)
            sp.dma_start(st[TILES:TILES + EXTRAS], xbf[0:EXTRAS]).then_inc(steps_out, 16)
            sp.dma_start(windowD[TILES:TILES + EXTRAS], tcoli[0:EXTRAS, 5:6]).then_inc(steps_out, 16)
            npad = STEPS + LOOK - TILES - EXTRAS
            sp.dma_start(stepsD[TILES + EXTRAS:STEPS + LOOK], padbf[0:npad]).then_inc(steps_out, 16)
            sp.dma_start(windowD[TILES + EXTRAS:STEPS + LOOK], tcoli[0:npad, 6:7]).then_inc(steps_out, 16)
            sp.wait_ge(steps_out, 8 * 16)
            sp.dma_start(window[:, :], windowD.rearrange("s a -> a s")).then_inc(window_loaded, 16)
            sp.wait_ge(extra_attr, 32)
            sp.dma_start(attrD[x0:x1, :].rearrange("(w e) f -> w (e f)", e=P), xattr[0:EXTRAS, :]
                         ).then_inc(tail_ready, 16)

            def put_table(l):
                sp.wait_ge(h_ready, l + 1)
                sp.dma_start(tableD[l].rearrange("(p b) f -> p (b f)", p=P),
                             h[:, :, :].rearrange("p b f -> p (b f)")).then_inc(table_out[l], 16)

            put_table(0)
            with sp.Fori(0, MAIN) as i:
                for k in range(2):
                    sp.wait_ge(row_used[k], i + 1)
                    sp.dma_start(attr[:, k], edge_attr[bass.ds(i * (BODY * P) + k * HB * P, HB * P), :]
                                 .rearrange("(u p) f -> p u f", p=P)).then_inc(attr_loaded[k], 16)
            sp.wait_ge(tail_ready, 4 * 16)
            with sp.Fori(0, C - MAIN) as i:
                for k in range(2):
                    sp.wait_ge(row_used[k], i + (MAIN + 1))
                    sp.dma_start(attr[:, k], attrD[bass.ds(i * (BODY * P) + k * HB * P, HB * P), :]
                                 .rearrange("(u p) f -> p u f", p=P)).then_inc(attr_loaded[k], 16)

            t1 = tableD[1].rearrange("(p b) f -> p b f", p=P)
            for b in range(0, BLOCKS, 2):
                sp.wait_ge(p1_copied, b + 2)
                sp.wait_ge(p1_biased, b + 2)
                sp.dma_start(t1[:, b:b + 2, :], trow[:, b % 4:b % 4 + 2, :]).then_inc(p1_out[b // 2 % 2], 16)

            def step_rows(i, k):
                sp.wait_ge(sel_ready[k], i + 1)
                sp.dma_start(rowb[:, k].rearrange("p u a e -> p (u a e)"),
                             stepsD[bass.ds(i * BODY + k * HB, HB), :].rearrange("s f -> (s f)").partition_broadcast(P)
                             ).then_inc(steps_loaded[k], 16)

            with sp.Fori(0, C) as i:
                for k in range(2):
                    step_rows(i, k)
            sp.wait_ge(sel_ready[0], C + 1)
            sp.dma_start(rowb[:, 0].rearrange("p u a e -> p (u a e)"),
                         stepsD[STEPS:STEPS + LOOK, :].rearrange("s f -> (s f)").partition_broadcast(P)
                         ).then_inc(steps_loaded[0], 16)

            put_table(2)
            put_table(3)
            sp.wait_ge(h_ready, 5)
            nb = BLOCKS - 1
            sp.dma_start(out[0:nb * P, :].rearrange("(b p) f -> p b f", p=P), x[:, 0:nb, :]).then_inc(stored, 16)
            sp.dma_start(out[nb * P:N_NODES, :], x[0:LAST_NODES, nb, :]).then_inc(stored, 16)
            sp.wait_ge(stored, 32)

        @block.gpsimd
        def _(pool):
            last = slice(FULL_CH, ROWCH)
            pool.memset(raw[:, 0:2, last, :], int(FAR)).then_inc(pads_set, 1)
            pool.memset(raw[:, 2:4, last, :], 0).then_inc(pads_set, 1)
            pool.memset(rows[:, last, WGT, :], 0.0).then_inc(pads_set, 1)
            pool.memset(x[:, BLOCKS - 1, :], 0.0).then_inc(pads_set, 1)
            pool.iota(iota_i[:, :], pattern=[[1, P]], base=0, channel_multiplier=0).then_inc(pads_set, 1)
            pool.iota(part_i[:, :], pattern=[[0, 1]], base=0, channel_multiplier=1).then_inc(pads_set, 1)
            pool.memset(ident[:, :], 0.0).then_inc(ident_ready, 1)
            pool.wait_ge(ident_ready, 1)
            pool.affine_select(out=ident[:, :], in_=ident[:, :], compare_op=ALU.not_equal, fill=1.0, base=0,
                               pattern=[[-1, P]], channel_multiplier=1).then_inc(ident_ready, 1)

            pool.wait_ge(extra_ready, 1)
            pool.wait_ge(rows_out, 16)
            pool.indirect_dma_start(out=xrow[0:EXTRAS].rearrange("p a e -> p (a e)"), out_offset=None, in_=rowsD,
                                    in_offset=bass.IndirectOffsetOnAxis(ap=tcoli[0:EXTRAS, 0:1], axis=0)
                                    ).then_inc(extra_rows, 16)
            halves = edge_attr.rearrange("(r e) f -> r (e f)", e=HALF)
            for k in range(2):
                pool.indirect_dma_start(out=xattr[0:EXTRAS, k * HALF * D:(k + 1) * HALF * D], out_offset=None,
                                        in_=halves,
                                        in_offset=bass.IndirectOffsetOnAxis(ap=tcoli[0:EXTRAS, 1 + k:2 + k], axis=0)
                                        ).then_inc(extra_attr, 16)

            for l in range(4):
                to = g1 if l == 1 else grow
                written = (table_out[l], 16)
                if l == 1:
                    lots = BLOCKS // 2
                    pool.wait_ge(p1_out[1], 16 * (lots // 2))
                    written = (p1_out[0], 16 * (lots - lots // 2))
                with pool.Fori(l * C + 1, (l + 1) * C + 1) as n:
                    for k in range(2):
                        pool.wait_ge(written[0], written[1])
                        pool.wait_ge(idx_ready[k], n)
                        pool.wait_ge((row_used, row_used, msg_ready, mm_done)[l][k], n)
                        for u in range(HB):
                            pool.indirect_dma_start(
                                out=to[:, k, u, :], out_offset=None, in_=tableD[l],
                                in_offset=bass.IndirectOffsetOnAxis(ap=idx[:, k, u:u + 1], axis=0)
                            ).then_inc(gathered[l][k], 16)

        @block.scalar
        def _(act):
            nb = BLOCKS - 1
            act.dma_start(x[:, 0:nb, :], x_in[0:nb * P, :].rearrange("(b p) f -> p b f", p=P)).then_inc(loaded, 16)
            act.wait_ge(pads_set, 4)
            act.dma_start(x[0:LAST_NODES, nb, :], x_in[nb * P:N_NODES, :]).then_inc(loaded, 16)
            act.wait_ge(consts, 9)
            for j in range(4):
                q = slice(j * D, (j + 1) * D)
                act.dma_start(nat[q, 0, q], W0).then_inc(loaded, 16)
                act.dma_start(nat[q, 1, q], W3).then_inc(loaded, 16)
                act.dma_start(wdiag[q, 1, q], W2).then_inc(loaded, 16)
                act.dma_start(wnat[q, 0:BASES, :], W1.rearrange("b i o -> i b o")).then_inc(loaded, 16)
                act.dma_start(wnat[q, BASES, :], wself).then_inc(loaded, 16)
                act.dma_start(anat[:, 0, j, :], A1).then_inc(loaded, 16)
                act.dma_start(anat[:, 1, j, :], A2).then_inc(loaded, 16)
                row = bias1[j * D:j * D + 1, MSG // 2:]
                act.dma_start(row[:, 0:D], A1b.rearrange("(a f) -> a f", a=1)).then_inc(loaded, 16)
                act.dma_start(row[:, D:], A2b.rearrange("(a f) -> a f", a=1)).then_inc(loaded, 16)
            for k, b in enumerate((b0, b2, b3)):
                act.dma_start(biasrow[:, k, :].rearrange("a (r f) -> a r f", f=D),
                              b.rearrange("(a f) -> a f", a=1).unsqueeze(1).to_broadcast([1, BANK // D, D])
                              ).then_inc(loaded, 16)
            act.dma_start(relc[0:RELS, 0:BASES], wcomp).then_inc(loaded, 16)
            act.dma_start(relc[0:RELS, BASES:YC], relemb).then_inc(loaded, 16)
            act.dma_start(opeps[:, :], eps0.partition_broadcast(P)).then_inc(loaded, 16)

            def norm(l):
                act.wait_ge(var_ready, l + 1)
                nc.scalar.activation(small[:, 2], small[:, 1], ACT.Sqrt).then_inc(std_ready, 1)

            norm(0)

            for c in range(ROWCH + 1):
                n = P if c < FULL_CH else TILES - FULL_CH * P if c == FULL_CH else EXTRAS
                at = c * P if c <= FULL_CH else TILES
                act.wait_ge(tabs_T, c + 1)
                bank = ps[:, (c % 7) * BANK:(c % 7 + 1) * BANK].rearrange("p (a e) -> p a e", a=4)
                nc.scalar.copy(tabs[:, :, at:at + n], bank[:, :, 0:n]).then_inc(tabs_copied, 1)

            def transposes(q):
                for b in range(BANKS):
                    w = min(BANK, GROUPS * P - b * BANK)
                    rows_ = P if b < BANKS - 1 else 2 * D
                    act.wait_ge(hT_done, BANKS * q + b + 1)
                    nc.scalar.copy(tT[0:rows_, b * BANK:b * BANK + w], ps[0:rows_, b * BANK:b * BANK + w]
                                   ).then_inc(hT_copied, 1)

            def lot(i, k):
                nc.scalar.copy(idx[:, k, :], srcT[:, bass.ds(i * BODY + k * HB, HB)]).then_inc(idx_ready[k], 1)

            def lots(l):
                with act.Fori(0, C) as i:
                    for k in range(2):
                        act.wait_ge(gathered[l][k], i * 64 + 64)
                        lot(i + 1, k)

            act.wait_ge(tabs_ready, 1)
            for k in range(2):
                lot(0, k)
            lots(0)
            transposes(0)
            norm(1)
            transposes(1)
            for b in range(BLOCKS):
                act.wait_ge(p1_done, b + 1)
                if b >= 4:
                    act.wait_ge(p1_out[b // 2 % 2], 16 * (b // 4))
                nc.scalar.copy(trow[:, b % 4, 0:MSG // 2], ps[:, (b % 4) * 2 * BANK:(b % 4) * 2 * BANK + MSG // 2]
                               ).then_inc(p1_copied, 1)

            def copy_yc(i, k, n):
                act.wait_ge(yc_done[k], i + 2)
                act.wait_ge(coef_ready[k], i + 1)
                nc.scalar.copy(yc[:, k], ps7).then_inc(yc_copied, 1)

            copy_yc(0, 0, 0)
            with act.Fori(0, C) as i:
                for k in range(2):
                    copy_yc(i + k, 1 - k, None)
                    act.wait_ge(score_ready[k], i + 1)
                    nc.scalar.activation(pos[:, k], score[:, k], ACT.Relu, scale=float(D) ** -0.5).then_inc(pos_ready, 1)
                    act.wait_ge(pos_ready, i * 2 + (k + 1))
                    nc.scalar.activation(att[:, k], pos[:, k], ACT.Tanh).then_inc(att_ready[k], 1)
                    act.wait_ge(gathered[1][k], i * 64 + 64)
                    lot(i + 1, k)
            norm(2)
            lots(2)
            transposes(2)
            norm(3)
            lots(3)
            transposes(3)

        @block.vector
        def _(dve):
            chain = [0]

            def step(ins):
                chain[0] += 1
                ins.then_inc(dve_chain, 1)
                dve.wait_ge(dve_chain, chain[0])

            tt, ts, cp = nc.vector.tensor_tensor, nc.vector.tensor_scalar, nc.vector.tensor_copy

            nc.vector.memset(nat[:, :, :], 0.0).then_inc(consts, 1)
            nc.vector.memset(wdiag[:, 1, :], 0.0).then_inc(consts, 1)
            nc.vector.memset(relc[:, :], 0.0).then_inc(consts, 1)
            nc.vector.memset(bias1[:, :], 0.0).then_inc(consts, 1)
            nc.vector.memset(zeros[:, :], 0.0).then_inc(consts, 1)
            nc.vector.memset(ones[:, :], 1.0).then_inc(consts, 1)
            nc.vector.memset(padbf[:, 0:P], FAR).then_inc(consts, 1)
            nc.vector.memset(padbf[:, P:2 * P], 0.0).then_inc(consts, 1)
            nc.vector.memset(tcoli[:, 6:7], 0).then_inc(consts, 1)
            nc.vector.memset(tabs[:, 1:4, TILES + EXTRAS:STEPS], 0.0)
            nc.vector.memset(tabs[:, 0, TILES + EXTRAS:STEPS], FAR)
            free = [s[k] for s in (row_used, msg_ready, mm_done, sel_ready, yc_done, coef_ready) for k in range(2)] + [yc_copied]
            for n, s in enumerate(free):
                nc.vector.memset(msg[:, 0, 0, n:n + 1], 0.0).then_inc(s, 1)
            dve.wait_ge(pads_set, 6)
            cp(iota[:, :], iota_i[:, :])
            step(cp(part[:, :], part_i[:, :]))
            step(nc.vector.tensor_scalar_add(part1[:, :], part[:, :], 1.0))
            step(ts(thr[:, :], iota[:, 0:EXTRAS], 1.0, float(P), ALU.add, ALU.mult))

            dve.wait_ge(edges_loaded, 15 * 16)
            dI, nI, sI, eI = (raw[:, a] for a in range(4))
            cp(rows[:, :, DLOC, :], dI)
            step(tt(rows[:, :, LAST, :], dI, nI, ALU.not_equal))
            step(cp(rows[:, :, ETY, :], eI))
            nc.vector.tensor_single_scalar(firstwi[:, 0, :], dI[:, :, 0], 7, ALU.arith_shift_right)
            step(nc.vector.tensor_single_scalar(nI, sI, P - 1, ALU.bitwise_and))
            step(nc.vector.tensor_single_scalar(eI, sI, 7, ALU.arith_shift_right))
            ins = nc.vector.scalar_tensor_tensor(rows[:, :, SRC, :], nI, float(BLOCKS), eI, ALU.mult, ALU.add)
            ins.then_inc(rows_ready, 1)
            step(cp(firstw[:, 0, :], firstwi[:, 0, :]))
            for c in range(ROWCH):
                last = ts(before[:, c, :], thr[:, :], rows[:, c, DLOC, P - 1:P], None, ALU.is_gt)
            last.then_inc(before_ready, 1)
            nc.vector.tensor_single_scalar(firstw[:, 1, :], firstw[:, 0, :], float(P), ALU.mult)
            step(nc.vector.tensor_single_scalar(firstwi[:, 1, :], firstw[:, 0, :], float(D), ALU.mult))
            tt(rloc[:, :, :], rows[:, :, DLOC, :], firstw[:, 1, :].unsqueeze(2).to_broadcast([P, ROWCH, P]), ALU.subtract)
            step(cp(rbf[:, :, 1, :], rows[:, :, ETY, :]))
            cp(rbf[:, :, 0, :], rloc[:, :, :]).then_inc(local_ready, 1)
            dve.wait_ge(count_done, 1)
            X = slice(0, EXTRAS)
            step(cp(tcol[X, 0:1], ps[X, 7 * BANK:7 * BANK + 1]))
            cp(tcoli[X, 0:1], tcol[X, 0:1])
            nc.vector.tensor_single_scalar(tcoli[X, 1:2], tcol[X, 0:1], 2.0, ALU.mult)
            step(ts(tcol[X, 1:2], tcol[X, 0:1], 2.0, 1.0, ALU.mult, ALU.add))
            nc.vector.tensor_single_scalar(tcoli[X, 2:3], tcol[X, 1:2], float(N_EDGES // HALF - 1), ALU.min
                                           ).then_inc(extra_ready, 1)

            dve.wait_ge(loaded, 44 * 16)
            step(nc.vector.tensor_scalar_add(opeps[:, :], opeps[:, :], 1.0))
            cp(wq[:, 0:MSG].rearrange("p (o b) -> p o b", o=D), wnat[:, :, :].rearrange("p b o -> p o b"))
            dve.wait_ge(wts_T, 1)
            cp(wdiag[:, 0, :], ps[:, 0:P])
            cp(wdiag[:, 2, :], ps[:, P:2 * P])
            cp(wq[:, MSG:MSG + 2 * D], ps[:, 2 * P:2 * P + 2 * D]).then_inc(wts_ready, 1)

            def norm(l):
                mean, var, std, r, a, b_ = (small[:, k] for k in range(6))
                wide = lambda v: v.unsqueeze(2).to_broadcast([P, BLOCKS, D])
                step(nc.vector.reduce_sum(mean, x[:, :, :], AX.X))
                step(nc.vector.tensor_single_scalar(mean, mean, 1.0 / D, ALU.mult))
                step(tt(h[:, :, :], x[:, :, :], wide(mean), ALU.subtract))
                step(tt(t[:, :, :], h[:, :, :], h[:, :, :], ALU.mult))
                step(nc.vector.reduce_sum(var, t[:, :, :], AX.X))
                ts(var, var, 1.0 / D, EPS, ALU.mult, ALU.add).then_inc(var_ready, 1)
                dve.wait_ge(std_ready, l + 1)
                step(nc.vector.reciprocal(r, std))
                step(tt(a, r, r, ALU.mult))
                step(tt(b_, a, var, ALU.mult))
                step(ts(a, b_, -0.5, 1.5, ALU.mult, ALU.add))
                step(tt(b_, a, r, ALU.mult))
                nc.vector.scalar_tensor_tensor(h[:, :, :], h[:, :, :], 0.0, wide(b_), ALU.max, ALU.mult
                                               ).then_inc(h_ready, 1)
                dve.wait_ge(h_ready, l + 1)

            norm(0)

            dve.wait_ge(extra_rows, 16)
            step(cp(tcoli[X, 3:4], xrow[X, DLOC, 0:1]))
            step(nc.vector.tensor_single_scalar(tcoli[X, 4:5], tcoli[X, 3:4], 7, ALU.arith_shift_right))
            step(cp(tcol[X, 4:5], tcoli[X, 4:5]))
            step(tt(tcol[X, 5:6], tcol[X, 4:5], part1[X, :], ALU.is_equal))
            nc.vector.tensor_single_scalar(tcoli[X, 5:6], part1[X, :], float(D), ALU.mult)
            step(nc.vector.tensor_single_scalar(tcol[X, 6:7], tcol[X, 5:6], FAR, ALU.mult))
            step(nc.vector.scalar_tensor_tensor(tcol[X, 7:8], part1[X, :], -float(P), tcol[X, 6:7], ALU.mult, ALU.add))
            step(ts(xloc[X, :], xrow[X, DLOC, :], tcol[X, 7:8], None, ALU.add))
            cp(xbf[X, 0, :], xloc[X, :])
            cp(xbf[X, 1, :], xrow[X, ETY, :]).then_inc(xlocal_ready, 1)
            dve.wait_ge(tabs_copied, ROWCH + 1)
            cp(srcT[:, STEPS:STEPS + BODY], tabs[:, SRC, 0:BODY])
            cp(srcT[:, 0:STEPS], tabs[:, SRC, :]).then_inc(tabs_ready, 1)

            def onehots(l, i, k):
                dve.wait_ge(mm_done[k], i + (l * C + 1))
                return tt(onehot[:, k], iota[:, :].unsqueeze(1).to_broadcast([P, HB, P]),
                          tabs[:, DLOC, bass.ds(i * BODY + k * HB, HB)].unsqueeze(2).to_broadcast([P, HB, P]),
                          ALU.is_equal)

            def per_edge(v, i, k, n):
                return tabs[:, v, bass.ds(i * BODY + k * HB, HB)].unsqueeze(2).to_broadcast([P, HB, n])

            with dve.Fori(0, C) as i:
                for k in range(2):
                    dve.wait_ge(gathered[0][k], i * 64 + 64)
                    dve.wait_ge(attr_loaded[k], i * 16 + 16)
                    dve.wait_ge(mm_done[k], i + 1)
                    tt(total[:, k], grow[:, k], attr[:, k], ALU.add).then_inc(row_used[k], 1)
                    onehots(0, i, k)
                    dve.wait_ge(row_used[k], i + 2)
                    nc.vector.tensor_single_scalar(msg[:, k], total[:, k], 0.0, ALU.max).then_inc(msg_ready[k], 1)

            def residual(q, relu):
                xf = x[:, :, :].rearrange("p b f -> p (b f)")
                for b in range(BANKS):
                    w = slice(b * BANK, min((b + 1) * BANK, FEAT))
                    dve.wait_ge(lin_done, BANKS * q + b + 1)
                    if relu:
                        ins = nc.vector.scalar_tensor_tensor(xf[:, w], ps[:, w], 0.0, xf[:, w], ALU.max, ALU.add)
                    else:
                        ins = tt(xf[:, w], ps[:, w], xf[:, w], ALU.add)
                step(ins)

            tf, hf = (v[:, :, :].rearrange("p b f -> p (b f)") for v in (t, h))

            def scattered(l):
                for k in range(2):
                    dve.wait_ge(mm_done[k], (l + 1) * C + 1)

            scattered(0)
            nc.vector.scalar_tensor_tensor(tf, hf, opeps[:, 0:1], acc, ALU.mult, ALU.add).then_inc(t_ready, 1)
            residual(0, False)
            norm(1)
            yf = y[:, :, :].rearrange("p b f -> p (b f)")
            for b in range(BLOCKS):
                at = (b % 4) * 2 * BANK + BANK
                dve.wait_ge(p1_done, b + 1)
                cp(yf[:, b * D:(b + 1) * D], ps[:, at + MSG // 2 + D:at + MSG // 2 + 2 * D])
                if b >= 4:
                    dve.wait_ge(p1_out[b // 2 % 2], 16 * (b // 4))
                cp(trow[:, b % 4, MSG // 2:ROW1], ps[:, at:at + MSG // 2 + D]).then_inc(p1_biased, 1)

            def selectors(i, k):
                dve.wait_ge(steps_loaded[k], i * 16 + 16)
                dve.wait_ge(yc_done[k], i + 1)
                ts(nodeT[:, k], rowb[:, k, :, 0, :], part[:, 0:1], None, ALU.is_equal)
                ts(relT[:, k], rowb[:, k, :, 1, :], part[:, 0:1], None, ALU.is_equal).then_inc(sel_ready[k], 1)

            selectors(0, 0)
            with dve.Fori(0, C) as i:
                for k in range(2):
                    dve.wait_ge(gathered[1][k], i * 64 + 64)
                    dve.wait_ge(yc_copied, i * 2 + (k + 2))
                    tt(yprod[:, :, :], g1[:, k, :, MSG:ROW1], yc[:, k, :, BASES:YC], ALU.mult).then_inc(yprod_ready, 1)
                    onehots(1, i, k)
                    cp(coef[:, :, BASES:BAS1], tabs[:, LAST, bass.ds(i * BODY + k * HB, HB)].unsqueeze(2))
                    dve.wait_ge(yprod_ready, i * 2 + (k + 1))
                    nc.vector.reduce_sum(score[:, k], yprod[:, :, :], AX.X).then_inc(score_ready[k], 1)
                    selectors(i + k, 1 - k)
                    dve.wait_ge(att_ready[k], i + 1)
                    tt(coef[:, :, 0:BASES], yc[:, k, :, 0:BASES], att[:, k].unsqueeze(2).to_broadcast([P, HB, BASES]),
                       ALU.mult).then_inc(coef_ready[k], 1)
                    dve.wait_ge(coef_ready[k], i + 2)
                    dve.wait_ge(msg_ready[1 - k], i + (C + 1 + k))
                    tt(prod[:, :, :, :], g1[:, k, :, 0:MSG].rearrange("p u (o b) -> p u o b", o=D),
                       coef[:, :, :].unsqueeze(2).to_broadcast([P, HB, D, BAS1]), ALU.mult).then_inc(row_used[k], 1)
                    dve.wait_ge(row_used[k], i + (C + 2))
                    nc.vector.reduce_sum(msg[:, k], prod[:, :, :, :], AX.X).then_inc(msg_ready[k], 1)
            scattered(1)
            step(nc.vector.scalar_tensor_tensor(x[:, :, :].rearrange("p b f -> p (b f)"), acc, 0.0,
                                                x[:, :, :].rearrange("p b f -> p (b f)"), ALU.max, ALU.add))
            norm(2)

            with dve.Fori(0, C) as i:
                for k in range(2):
                    onehots(2, i, k)
                    dve.wait_ge(gathered[2][k], i * 64 + 64)
                    tt(msg[:, k], grow[:, k], per_edge(WGT, i, k, D), ALU.mult).then_inc(msg_ready[k], 1)
            scattered(2)
            cp(tf, acc).then_inc(t_ready, 1)
            residual(1, True)
            norm(3)

            with dve.Fori(0, C) as i:
                for k in range(2):
                    onehots(3, i, k).then_inc(msg_ready[k], 1)
            scattered(3)
            cp(tf, acc).then_inc(t_ready, 1)
            residual(2, False)
            nc.vector.tensor_copy(total[:, 0, 0, 0:1], x[:, 0, 0:1]).then_inc(h_ready, 1)

        @block.tensor
        def _(pe):
            mm = nc.tensor.matmul
            pe.wait_ge(consts, 9)
            pe.wait_ge(ident_ready, 2)
            pe.wait_ge(before_ready, 1)
            for c in range(ROWCH):
                last = mm(ps[0:EXTRAS, 7 * BANK:7 * BANK + 1], before[:, c, :], ones[:, 0:1], start=(c == 0),
                          stop=(c == ROWCH - 1))
            last.then_inc(count_done, 1)
            pe.wait_ge(loaded, 44 * 16)
            nc.tensor.transpose(ps[:, 0:P], nat[:, 0, :], ident[:, :])
            nc.tensor.transpose(ps[:, P:2 * P], nat[:, 1, :], ident[:, :])
            nc.tensor.transpose(ps[:, 2 * P:2 * P + D], anat[:, 0].rearrange("o r i -> o (r i)"), ident[0:D, 0:D])
            nc.tensor.transpose(ps[:, 2 * P + D:2 * P + 2 * D], anat[:, 1].rearrange("o r i -> o (r i)"),
                                ident[0:D, 0:D]).then_inc(wts_T, 1)
            pe.wait_ge(wts_ready, 1)

            pe.wait_ge(local_ready, 1)
            for c in range(ROWCH + 1):
                n = P if c < FULL_CH else TILES - FULL_CH * P if c == FULL_CH else EXTRAS
                if c > FULL_CH:
                    pe.wait_ge(xlocal_ready, 1)
                if c >= 7:
                    pe.wait_ge(tabs_copied, c - 6)
                for a in range(4):
                    of = (xloc[0:n, :] if c > FULL_CH else rloc[0:n, c, :]) if a == DLOC else \
                        xrow[0:n, a, :] if c > FULL_CH else rows[0:n, c, a, :]
                    at = (c % 7) * BANK + a * P
                    last = nc.tensor.transpose(ps[:, at:at + n], of, ident[0:n, 0:n])
                last.then_inc(tabs_T, 1)
            pe.wait_ge(tabs_copied, ROWCH + 1)
            pe.wait_ge(window_loaded, 16)

            def clear():
                for b in range(BANKS):
                    mm(ps[:, b * BANK:(b + 1) * BANK], zeros[0:1, 0:P], zeros[0:1, :], start=True, stop=True,
                       skip_group_check=True)

            def windows(i, n, first=0):
                _, w = nc.values_load_multi_w_load_instructions(
                    window[0:1, bass.ds(i * BODY + first, n)], engines=(mybir.EngineType.PE,), min_val=0,
                    max_val=(BLOCKS - 1) * D, skip_runtime_bounds_check_because="windows of nodes below N_NODES")
                return w

            def scatter(l, i, k, w, of):
                pe.wait_ge(msg_ready[k], i + (l * C + 2))
                for u in range(HB):
                    last = mm(ps[:, bass.ds(w[u], D)], onehot[:, k, u, :], of[:, k, u, :], start=False, stop=True,
                              skip_group_check=True)
                last.then_inc(mm_done[k], 1)

            def transposes(of):
                for b in range(BANKS):
                    for g in range(4 * b, min(4 * b + 4, GROUPS)):
                        n = min(P, FEAT - g * P)
                        last = nc.tensor.transpose(ps[0:n, g * P:(g + 1) * P], of[:, g * P:g * P + n], ident[:, :])
                    last.then_inc(hT_done, 1)

            tf, hf = (v[:, :, :].rearrange("p b f -> p (b f)") for v in (t, h))

            def linear(q, copies, w, bias):
                pe.wait_ge(t_ready, q + 1)
                transposes(tf)
                for b in range(BANKS):
                    n = min(BANK, FEAT - b * BANK)
                    pe.wait_ge(hT_copied, BANKS * (copies + 1) if b == 0 else BANKS * copies + b + 1)
                    mm(ps[:, b * BANK:b * BANK + n], ones[0:1, :], biasrow[:, bias, 0:n], start=True, stop=False,
                       skip_group_check=True)
                    for g in range(4 * b, min(4 * b + 4, GROUPS)):
                        m = min(P, FEAT - g * P)
                        last = mm(ps[:, g * P:g * P + m], tT[0:m, g * P:(g + 1) * P], wdiag[0:m, w, 0:m],
                                  start=False, stop=True, skip_group_check=True)
                    last.then_inc(lin_done, 1)

            clear()
            with pe.Fori(0, C) as i:
                w = windows(i, BODY)
                for k in range(2):
                    scatter(0, i, k, w[k * HB:], msg)
            linear(0, 0, 0, 0)

            pe.wait_ge(h_ready, 2)
            pe.wait_ge(lin_done, BANKS)
            transposes(hf)
            pe.wait_ge(hT_copied, 2 * BANKS)
            for b in range(BLOCKS):
                g, j, at = b // 4, b % 4, (b % 4) * 2 * BANK
                if b >= 4:
                    pe.wait_ge(p1_copied, b - 3)
                    pe.wait_ge(p1_biased, b - 3)
                q = slice(j * D, (j + 1) * D)
                lhsT = tT[q, g * P:(g + 1) * P]
                mm(ps[:, at:at + MSG // 2], lhsT, wq[q, 0:MSG // 2], start=True, stop=True)
                two = ps[:, at + BANK:at + BANK + MSG // 2 + 2 * D]
                mm(two, ones[j * D:j * D + 1, :], bias1[j * D:j * D + 1, :], start=True, stop=False)
                mm(two, lhsT, wq[q, MSG // 2:MSG + 2 * D], start=False, stop=True).then_inc(p1_done, 1)
            pe.wait_ge(p1_copied, BLOCKS)
            pe.wait_ge(p1_biased, BLOCKS)
            clear()

            def edge_terms(i, k, w, n):
                pe.wait_ge(sel_ready[k], i + 2)
                pe.wait_ge(yc_copied, n)
                for u in range(HB):
                    mm(ps7[:, u, :], relT[:, k, u, :], relc[:, :], start=True, stop=False, skip_group_check=True)
                    last = mm(ps7[:, u, BASES:YC], nodeT[:, k, u, :], yf[:, bass.ds(w[u], D)], start=False, stop=True,
                              skip_group_check=True)
                last.then_inc(yc_done[k], 1)

            yf = tf
            edge_terms(0, 0, windows(0, HB), 1)
            with pe.Fori(0, C) as i:
                w = windows(i, BODY + HB)
                for k in range(2):
                    edge_terms(i + k, 1 - k, w[(k + 1) * HB:], i * 2 + (k + 2))
                    scatter(1, i, k, w[k * HB:], msg)
            pe.wait_ge(h_ready, 3)
            clear()
            with pe.Fori(0, C) as i:
                w = windows(i, BODY)
                for k in range(2):
                    scatter(2, i, k, w[k * HB:], msg)
            linear(1, 2, 1, 1)
            pe.wait_ge(h_ready, 4)
            clear()
            with pe.Fori(0, C) as i:
                w = windows(i, BODY)
                for k in range(2):
                    pe.wait_ge(gathered[3][k], i * 64 + 64)
                    scatter(3, i, k, w[k * HB:], grow)
            linear(2, 3, 2, 2)


_INS = ['x', 'src', 'dst', 'edge_attr_32', 'edge_type_86', 'edge_weight', 'L0_gnn_W', 'L0_gnn_b', 'L0_gnn_eps',
        'L1_gnn_weight', 'L1_gnn_w_comp', 'L1_gnn_self_loop_weight', 'L1_gnn_A1_w', 'L1_gnn_A1_b', 'L1_gnn_A2_w',
        'L1_gnn_A2_b', 'L1_gnn_rel_emb', 'L2_gnn_W', 'L2_gnn_b', 'L3_gnn_W', 'L3_gnn_b']


def kernel(**inputs):
    import numpy as _np
    import concourse.bacc as _bacc
    from concourse import mybir as _mybir
    from concourse.bass_utils import run_bass_kernel_spmd as _run

    nc = _bacc.Bacc("TRN2", target_bir_lowering=False, num_devices=1)
    arrays, args = {}, []
    for name in _INS:
        a = _np.ascontiguousarray(inputs[name])
        arrays[f"in_{name}"] = a
        args.append(nc.dram_tensor(f"in_{name}", a.shape, _mybir.dt.from_np(a.dtype), kind="ExternalInput").ap())
    out = nc.dram_tensor("out_nodes", (N_NODES, D), F32, kind="ExternalOutput").ap()
    gnn(nc, *args, out)
    r = _run(nc, [arrays], core_ids=[0])
    return r.results[0]["out_nodes"]
```

```python
import concourse.bass as bass
from concourse import mybir
from contextlib import ExitStack

F32 = mybir.dt.float32
I32 = mybir.dt.int32
BF16 = mybir.dt.bfloat16
ALU = mybir.AluOpType
ACT = mybir.ActivationFunctionType
AX = mybir.AxisListType

P = 128
N_NODES, N_EDGES, D = 12500, 200000, 32
RELS, BASES = 86, 16
EPS = 1e-5

BLOCKS = -(-N_NODES // P)
LAST_NODES = N_NODES - (BLOCKS - 1) * P
TILES = -(-N_EDGES // P)
ROWCH = -(-TILES // P)
FULL_CH = TILES // P
TAIL_TILES = N_EDGES // P - FULL_CH * P
HALF = N_EDGES - (N_EDGES // P) * P
EXTRAS = BLOCKS - 1
LOTS, HB = 4, 4
BODY = LOTS * HB
STEPS = -(-(TILES + EXTRAS) // BODY) * BODY
C = STEPS // BODY
MAIN = (N_EDGES // P) // BODY
TAIL = STEPS - MAIN * BODY
P1_LOTS = -(-BLOCKS // 4)
FAR = float(1 << 20)
FEAT = BLOCKS * D
BANK = 512
GROUPS = -(-BLOCKS // 4)
BANKS = -(-FEAT // BANK)
BAS1 = BASES + 1
MSG = D * BAS1
ROW1 = MSG + D
YC = BASES + D


def gnn(nc, x_in, src, dst, edge_attr, etype, weight, W0, b0, eps0, W1, wcomp, wself, A1, A1b, A2, A2b,
        relemb, W2, b2, W3, b3, out):
    tableD = [nc.dram_tensor(f"table{l}", (BLOCKS * P, ROW1 if l == 1 else D), F32, kind="Internal").ap()
              for l in range(4)]
    rowsD = nc.dram_tensor("edge_rows", (ROWCH * P, 5 * P), F32, kind="Internal").ap()
    stepsD = nc.dram_tensor("step_rows", (STEPS, 2 * P), BF16, kind="Internal").ap()
    windowD = nc.dram_tensor("step_window", (STEPS, 1), I32, kind="Internal").ap()
    attrD = nc.dram_tensor("attr_tail", (TAIL * P, D), F32, kind="Internal").ap()

    ctx = ExitStack()
    with ctx:
        ctx.enter_context(nc.allow_non_contiguous_dma("small weights and window offsets"))

        def sb(name, shape, dt=F32):
            return ctx.enter_context(nc.sbuf_tensor(name, shape, dt))

        def sem(name):
            return ctx.enter_context(nc.semaphore(name))

        def lotwise(name):
            return [sem(f"{name}_{h}") for h in range(LOTS)]

        x = sb("x", [P, BLOCKS, D])
        h = sb("h", [P, BLOCKS, D])
        t = sb("t", [P, BLOCKS, D])
        tT = sb("tT", [P, GROUPS * P])
        tabs = sb("tabs", [P, 4, STEPS])
        DLOC, SRC, WGT, LAST, ETY = range(5)
        srcT = sb("srcT", [P, STEPS + BODY], I32)
        window = sb("window", [1, STEPS], I32)
        onehot = sb("onehot", [P, LOTS, HB, P])
        msg = sb("msg", [P, LOTS, HB, D])
        attr = sb("attr", [P, LOTS, HB, D])
        grow = sb("grow", [P, LOTS, HB, D])
        total = sb("total", [P, LOTS, HB, D])
        idx = sb("idx", [P, LOTS, HB], I32)
        iota_i = sb("iota_i", [P, P], I32)
        iota = sb("iota", [P, P])
        part_i = sb("part_i", [P, 1], I32)
        part = sb("part", [P, 1])
        part1 = sb("part1", [P, 1])
        thr = sb("thr", [P, EXTRAS])
        ident = sb("ident", [P, P])
        zeros = sb("zeros", [1, BANK])
        ones = sb("ones", [P, P])
        nat = sb("nat", [P, 2, P])
        wdiag = sb("wdiag", [P, 3, P])
        anat = sb("anat", [D, 2, 4, D])
        wq = sb("wq", [P, MSG + 2 * D])
        biasrow = sb("biasrow", [1, 3, BANK])
        bias1 = sb("bias1", [P, 2 * D])
        relc = sb("relc", [P, YC])
        relparts = sb("relparts", [P, 3, YC], BF16)
        relrest = sb("relrest", [P, 2, YC])
        opeps = sb("opeps", [P, 1])
        small = sb("small", [P, 6, BLOCKS])
        arena = sb("arena", [P, 19600])

        used = [0]

        def region(n, dt=F32):
            a = arena[:, used[0]:used[0] + n]
            used[0] += n
            return a if dt == F32 else a.bitcast(dt)

        raw = region(4 * ROWCH * P, I32).rearrange("p (a c e) -> p a c e", a=4, c=ROWCH)
        rows = region(ROWCH * 5 * P).rearrange("p (c a e) -> p c a e", c=ROWCH, a=5)
        rloc = region(ROWCH * P).rearrange("p (c e) -> p c e", c=ROWCH)
        rbf = region(ROWCH * P, BF16).rearrange("p (c a e) -> p c a e", c=ROWCH, a=2)
        xrow = region(5 * P).rearrange("p (a e) -> p a e", a=5)
        xattr = arena[:, 0:P * D]
        xloc = region(P)
        xbf = region(P, BF16).rearrange("p (a e) -> p a e", a=2)
        padbf = region(P, BF16)
        tcol = region(16)
        tcoli = region(16, I32)
        firstw = region(2 * ROWCH).rearrange("p (a c) -> p a c", a=2)
        firstwi = region(2 * ROWCH, I32).rearrange("p (a c) -> p a c", a=2)
        before = tT[:, 0:ROWCH * EXTRAS].rearrange("p (c w) -> p c w", c=ROWCH)
        wnat = tT[:, ROWCH * EXTRAS:ROWCH * EXTRAS + BAS1 * D].rearrange("p (b o) -> p b o", b=BAS1)
        used[0] = 0
        g1 = region(LOTS * HB * ROW1).rearrange("p (h u f) -> p h u f", h=LOTS, u=HB)
        prod = region(HB * MSG).rearrange("p (u o b) -> p u o b", u=HB, o=D)
        rowb = region(LOTS * HB * P, BF16).rearrange("p (h u a e) -> p h u a e", h=LOTS, u=HB, a=2)
        nodeT = region(LOTS * HB * P).rearrange("p (h u e) -> p h u e", h=LOTS, u=HB)
        relT = region(LOTS * HB * P // 2, BF16).rearrange("p (h u e) -> p h u e", h=LOTS, u=HB)
        off = region(HB * 2 * P).rearrange("p (u a e) -> p u a e", u=HB, a=2)
        yc = region(LOTS * HB * YC).rearrange("p (h u f) -> p h u f", h=LOTS, u=HB)
        yprod = region(HB * D).rearrange("p (u f) -> p u f", u=HB)
        coef = region(HB * BAS1).rearrange("p (u b) -> p u b", u=HB)
        score = region(LOTS * HB).rearrange("p (h u) -> p h u", h=LOTS)
        pos = region(LOTS * HB).rearrange("p (h u) -> p h u", h=LOTS)
        att = region(LOTS * HB).rearrange("p (h u) -> p h u", h=LOTS)
        away = region(HB * P).rearrange("p (u n) -> p u n", u=HB)
        trow = arena[:, 0:16 * ROW1].rearrange("p (r f) -> p r f", r=16)
        y = t

        ps = ctx.enter_context(nc.psum_tensor("ps", [P, 8 * BANK], F32))
        acc = ps[:, 0:FEAT]
        ps7 = ps[:, 7 * BANK:7 * BANK + HB * YC].rearrange("p (u f) -> p u f", u=HB)

        loaded = sem("inputs_loaded")
        edges_loaded = sem("edges_loaded")
        pads_set = sem("pads_set")
        consts = sem("consts_ready")
        ident_ready = sem("identity_ready")
        dve_chain = sem("dve_chain")
        act_chain = sem("act_chain")
        wts_T = sem("weights_transposed")
        wts_ready = sem("weights_ready")
        rows_ready = sem("rows_ready")
        rows_out = sem("rows_written")
        before_ready = sem("before_ready")
        count_done = sem("extra_tiles_counted")
        extra_ready = sem("extra_tiles_ready")
        extra_rows = sem("extra_rows_gathered")
        extra_attr = sem("extra_attr_gathered")
        local_ready = sem("local_nodes_ready")
        xlocal_ready = sem("extra_local_ready")
        tabs_T = sem("tables_transposed")
        tabs_copied = sem("tables_copied")
        tabs_ready = sem("tables_ready")
        steps_out = sem("steps_written")
        window_loaded = sem("window_loaded")
        tail_ready = sem("attr_tail_written")
        var_ready = sem("variance_ready")
        std_ready = sem("std_ready")
        h_ready = sem("h_ready")
        table_out = [sem(f"table_written_{l}") for l in range(4)]
        hT_done = sem("transposed")
        hT_copied = sem("transposes_copied")
        lin_done = sem("linear_done")
        t_ready = sem("t_ready")
        acc_free = sem("sums_read")
        idx_ready = lotwise("idx_ready")
        gathered = [lotwise(f"gathered{l}") for l in range(4)]
        row_used = lotwise("gathered_used")
        attr_loaded = lotwise("attr_loaded")
        summed = sem("edge_sum_ready")
        msg_ready = lotwise("msg_ready")
        mm_done = lotwise("scatter_done")
        p1_done = sem("node_products_done")
        p1_copied = sem("node_products_copied")
        p1_biased = sem("node_products_copied_by_vector")
        p1_out = lotwise("node_products_written")
        steps_loaded = lotwise("step_rows_loaded")
        sel_ready = lotwise("selectors_ready")
        yc_done = lotwise("yc_done")
        yc_copied = sem("yc_copied")
        yprod_ready = lotwise("yprod_ready")
        score_ready = lotwise("score_ready")
        pos_ready = lotwise("positive_score_ready")
        away_ready = lotwise("distance_ready")
        off_ready = lotwise("selector_distance_ready")
        node_sel_ready = lotwise("node_selector_ready")
        onehot_ready = lotwise("onehot_ready")
        att_ready = lotwise("attention_ready")
        coef_ready = lotwise("coef_ready")
        stored = sem("output_stored")

        block = ctx.enter_context(nc.Block())

        @block.sync
        def _(sp):
            n_full = FULL_CH * P * P
            n_tail = n_full + TAIL_TILES * P
            sp.wait_ge(pads_set, 4)

            def edge_rows(to, of, shift):
                sp.dma_start(to[:, 0:FULL_CH, :], of[shift:n_full + shift].rearrange("(c p e) -> p c e", p=P, e=P)
                             ).then_inc(edges_loaded, 16)
                sp.dma_start(to[0:TAIL_TILES, FULL_CH, :],
                             of[n_full + shift:n_tail + shift].rearrange("(p e) -> p e", e=P)
                             ).then_inc(edges_loaded, 16)
                sp.dma_start(to[TAIL_TILES:TAIL_TILES + 1, FULL_CH, 0:HALF - shift],
                             of[n_tail + shift:N_EDGES].rearrange("(a e) -> a e", a=1)).then_inc(edges_loaded, 16)

            edge_rows(raw[:, 0], dst, 0)
            edge_rows(raw[:, 1], dst, 1)
            edge_rows(raw[:, 2], src, 0)
            edge_rows(raw[:, 3], etype, 0)
            edge_rows(rows[:, :, WGT, :], weight, 0)
            sp.dma_start(attrD[0:N_EDGES - MAIN * BODY * P, :], edge_attr[MAIN * BODY * P:N_EDGES, :]
                         ).then_inc(tail_ready, 16)
            at = N_EDGES - MAIN * BODY * P
            sp.dma_start(attrD[at:at + P - HALF, :], edge_attr[0:P - HALF, :]).then_inc(tail_ready, 16)
            x0 = at + P - HALF
            x1 = x0 + EXTRAS * P
            sp.dma_start(attrD[x1:TAIL * P, :], edge_attr[0:TAIL * P - x1, :]).then_inc(tail_ready, 16)

            sp.wait_ge(rows_ready, 1)
            sp.dma_start(rowsD.rearrange("(c p) f -> p c f", p=P), rows[:, :, :, :].rearrange("p c a e -> p c (a e)")
                         ).then_inc(rows_out, 16)
            sp.wait_ge(local_ready, 1)
            st = stepsD.rearrange("s (a e) -> s a e", a=2)
            sp.dma_start(st[0:FULL_CH * P].rearrange("(c p) a e -> p c a e", p=P), rbf[:, 0:FULL_CH]
                         ).then_inc(steps_out, 16)
            sp.dma_start(st[FULL_CH * P:TILES], rbf[0:TILES - FULL_CH * P, FULL_CH]).then_inc(steps_out, 16)
            sp.dma_start(windowD[0:FULL_CH * P].rearrange("(c p) a -> p (c a)", p=P), firstwi[:, 1, 0:FULL_CH]
                         ).then_inc(steps_out, 16)
            sp.dma_start(windowD[FULL_CH * P:TILES], firstwi[0:TILES - FULL_CH * P, 1, FULL_CH:ROWCH]
                         ).then_inc(steps_out, 16)
            sp.wait_ge(xlocal_ready, 1)
            sp.dma_start(st[TILES:TILES + EXTRAS], xbf[0:EXTRAS]).then_inc(steps_out, 16)
            sp.dma_start(windowD[TILES:TILES + EXTRAS], tcoli[0:EXTRAS, 5:6]).then_inc(steps_out, 16)
            npad = STEPS - TILES - EXTRAS
            sp.dma_start(stepsD[TILES + EXTRAS:STEPS], padbf[0:npad]).then_inc(steps_out, 16)
            sp.dma_start(windowD[TILES + EXTRAS:STEPS], tcoli[0:npad, 6:7]).then_inc(steps_out, 16)
            sp.wait_ge(steps_out, 8 * 16)
            sp.dma_start(window[:, :], windowD.rearrange("s a -> a s")).then_inc(window_loaded, 16)
            sp.wait_ge(extra_attr, 32)
            sp.dma_start(attrD[x0:x1, :].rearrange("(w e) f -> w (e f)", e=P), xattr[0:EXTRAS, :]
                         ).then_inc(tail_ready, 16)

            def put_table(l):
                sp.wait_ge(h_ready, l + 1)
                sp.dma_start(tableD[l].rearrange("(p b) f -> p (b f)", p=P),
                             h[:, :, :].rearrange("p b f -> p (b f)")).then_inc(table_out[l], 16)

            put_table(0)
            with sp.Fori(0, MAIN) as i:
                for k in range(LOTS):
                    sp.wait_ge(row_used[k], i + 1)
                    sp.dma_start(attr[:, k], edge_attr[bass.ds(i * (BODY * P) + k * (HB * P), HB * P), :]
                                 .rearrange("(u p) f -> p u f", p=P)).then_inc(attr_loaded[k], 16)
            sp.wait_ge(tail_ready, 4 * 16)
            with sp.Fori(0, C - MAIN) as i:
                for k in range(LOTS):
                    sp.wait_ge(row_used[k], i + (MAIN + 1))
                    sp.dma_start(attr[:, k], attrD[bass.ds(i * (BODY * P) + k * (HB * P), HB * P), :]
                                 .rearrange("(u p) f -> p u f", p=P)).then_inc(attr_loaded[k], 16)

            t1 = tableD[1].rearrange("(p b) f -> p b f", p=P)
            for m in range(P1_LOTS):
                b, e = 4 * m, min(4 * m + 4, BLOCKS)
                sp.wait_ge(p1_copied, e)
                sp.wait_ge(p1_biased, e)
                sp.dma_start(t1[:, b:e, :], trow[:, b % 16:b % 16 + e - b, :]).then_inc(p1_out[m % LOTS], 16)

            with sp.Fori(0, C) as i:
                for k in range(LOTS):
                    sp.wait_ge(sel_ready[k], i + 1)
                    sp.dma_start(rowb[:, k].rearrange("p u a e -> p (u a e)"),
                                 stepsD[bass.ds(i * BODY + k * HB, HB), :].rearrange("s f -> (s f)")
                                 .partition_broadcast(P)).then_inc(steps_loaded[k], 16)

            put_table(2)
            put_table(3)
            sp.wait_ge(h_ready, 5)
            nb = BLOCKS - 1
            sp.dma_start(out[0:nb * P, :].rearrange("(b p) f -> p b f", p=P), x[:, 0:nb, :]).then_inc(stored, 16)
            sp.dma_start(out[nb * P:N_NODES, :], x[0:LAST_NODES, nb, :]).then_inc(stored, 16)
            sp.wait_ge(stored, 32)

        @block.gpsimd
        def _(pool):
            last = slice(FULL_CH, ROWCH)
            pool.memset(raw[:, 0:2, last, :], int(FAR)).then_inc(pads_set, 1)
            pool.memset(raw[:, 2:4, last, :], 0).then_inc(pads_set, 1)
            pool.memset(rows[:, last, WGT, :], 0.0).then_inc(pads_set, 1)
            pool.memset(x[:, BLOCKS - 1, :], 0.0).then_inc(pads_set, 1)
            pool.iota(iota_i[:, :], pattern=[[1, P]], base=0, channel_multiplier=0).then_inc(pads_set, 1)
            pool.iota(part_i[:, :], pattern=[[0, 1]], base=0, channel_multiplier=1).then_inc(pads_set, 1)
            pool.memset(ident[:, :], 0.0).then_inc(ident_ready, 1)
            pool.wait_ge(ident_ready, 1)
            pool.affine_select(out=ident[:, :], in_=ident[:, :], compare_op=ALU.not_equal, fill=1.0, base=0,
                               pattern=[[-1, P]], channel_multiplier=1).then_inc(ident_ready, 1)

            pool.wait_ge(extra_ready, 1)
            pool.wait_ge(rows_out, 16)
            pool.indirect_dma_start(out=xrow[0:EXTRAS].rearrange("p a e -> p (a e)"), out_offset=None, in_=rowsD,
                                    in_offset=bass.IndirectOffsetOnAxis(ap=tcoli[0:EXTRAS, 0:1], axis=0)
                                    ).then_inc(extra_rows, 16)
            halves = edge_attr.rearrange("(r e) f -> r (e f)", e=HALF)
            for k in range(2):
                pool.indirect_dma_start(out=xattr[0:EXTRAS, k * HALF * D:(k + 1) * HALF * D], out_offset=None,
                                        in_=halves,
                                        in_offset=bass.IndirectOffsetOnAxis(ap=tcoli[0:EXTRAS, 1 + k:2 + k], axis=0)
                                        ).then_inc(extra_attr, 16)

            for l in range(4):
                to = g1 if l == 1 else grow
                written = (table_out[l], 16)
                if l == 1:
                    for k in range(LOTS):
                        written = (p1_out[k], 16 * ((P1_LOTS - 1 - k) // LOTS + 1))
                        pool.wait_ge(*written)
                with pool.Fori(l * C + 1, (l + 1) * C + 1) as n:
                    for k in range(LOTS):
                        pool.wait_ge(written[0], written[1])
                        pool.wait_ge(idx_ready[k], n)
                        pool.wait_ge((row_used, row_used, msg_ready, mm_done)[l][k], n)
                        for u in range(HB):
                            pool.indirect_dma_start(
                                out=to[:, k, u, :], out_offset=None, in_=tableD[l],
                                in_offset=bass.IndirectOffsetOnAxis(ap=idx[:, k, u:u + 1], axis=0)
                            ).then_inc(gathered[l][k], 16)

        @block.scalar
        def _(act):
            nb = BLOCKS - 1
            act.dma_start(x[:, 0:nb, :], x_in[0:nb * P, :].rearrange("(b p) f -> p b f", p=P)).then_inc(loaded, 16)
            act.wait_ge(pads_set, 4)
            act.dma_start(x[0:LAST_NODES, nb, :], x_in[nb * P:N_NODES, :]).then_inc(loaded, 16)
            act.wait_ge(consts, 8)
            for j in range(4):
                q = slice(j * D, (j + 1) * D)
                act.dma_start(nat[q, 0, q], W0).then_inc(loaded, 16)
                act.dma_start(nat[q, 1, q], W3).then_inc(loaded, 16)
                act.dma_start(wdiag[q, 1, q], W2).then_inc(loaded, 16)
                act.dma_start(wnat[q, 0:BASES, :], W1.rearrange("b i o -> i b o")).then_inc(loaded, 16)
                act.dma_start(wnat[q, BASES, :], wself).then_inc(loaded, 16)
                act.dma_start(anat[:, 0, j, :], A1).then_inc(loaded, 16)
                act.dma_start(anat[:, 1, j, :], A2).then_inc(loaded, 16)
            act.dma_start(bias1[:, 0:D], A1b.partition_broadcast(P)).then_inc(loaded, 16)
            act.dma_start(bias1[:, D:], A2b.partition_broadcast(P)).then_inc(loaded, 16)
            for k, b in enumerate((b0, b2, b3)):
                act.dma_start(biasrow[:, k, :].rearrange("a (r f) -> a r f", f=D),
                              b.rearrange("(a f) -> a f", a=1).unsqueeze(1).to_broadcast([1, BANK // D, D])
                              ).then_inc(loaded, 16)
            act.dma_start(relc[0:RELS, 0:BASES], wcomp).then_inc(loaded, 16)
            act.dma_start(relc[0:RELS, BASES:YC], relemb).then_inc(loaded, 16)
            act.dma_start(opeps[:, :], eps0.partition_broadcast(P)).then_inc(loaded, 16)

            def norm(l):
                act.wait_ge(var_ready, l + 1)
                nc.scalar.activation(small[:, 2], small[:, 1], ACT.Sqrt).then_inc(std_ready, 1)

            norm(0)

            for c in range(ROWCH + 1):
                n = P if c < FULL_CH else TILES - FULL_CH * P if c == FULL_CH else EXTRAS
                at = c * P if c <= FULL_CH else TILES
                act.wait_ge(tabs_T, c + 1)
                bank = ps[:, (c % 7) * BANK:(c % 7 + 1) * BANK].rearrange("p (a e) -> p a e", a=4)
                nc.scalar.copy(tabs[:, :, at:at + n], bank[:, :, 0:n]).then_inc(tabs_copied, 1)

            def transposes(q):
                for b in range(BANKS):
                    w = min(BANK, GROUPS * P - b * BANK)
                    rows_ = P if b < BANKS - 1 else 2 * D
                    act.wait_ge(hT_done, BANKS * q + b + 1)
                    nc.scalar.copy(tT[0:rows_, b * BANK:b * BANK + w], ps[0:rows_, b * BANK:b * BANK + w]
                                   ).then_inc(hT_copied, 1)

            def lot(i, k):
                nc.scalar.copy(idx[:, k, :], srcT[:, bass.ds(i * BODY + k * HB, HB)]).then_inc(idx_ready[k], 1)

            def lots(l):
                with act.Fori(0, C) as i:
                    for k in range(LOTS):
                        act.wait_ge(gathered[l][k], i * 64 + 64)
                        lot(i + 1, k)

            act.wait_ge(tabs_ready, 1)
            for k in range(LOTS):
                lot(0, k)
            lots(0)
            transposes(0)
            norm(1)
            transposes(1)
            for b in range(BLOCKS):
                act.wait_ge(p1_done, b + 1)
                if b >= 16 and b % 4 == 0:
                    act.wait_ge(p1_out[b // 4 % LOTS], 16 * (b // 16))
                at = (b % 4) * 2 * BANK
                nc.scalar.copy(trow[:, b % 16, 0:MSG // 2], ps[:, at:at + MSG // 2]).then_inc(p1_copied, 1)

            def copy_yc(i, k):
                act.wait_ge(yc_done[k], i + 2)
                act.wait_ge(coef_ready[k], i + 1)
                nc.scalar.copy(yc[:, k], ps7).then_inc(yc_copied, 1)

            def attention(i, k):
                act.wait_ge(score_ready[k], i + 1)
                nc.scalar.activation(pos[:, k], score[:, k], ACT.Relu, scale=float(D) ** -0.5).then_inc(pos_ready[k], 1)
                act.wait_ge(pos_ready[k], i + 1)
                nc.scalar.activation(att[:, k], pos[:, k], ACT.Tanh).then_inc(att_ready[k], 1)

            def selectors(i, k):
                act.wait_ge(steps_loaded[k], i * 16 + 16)
                act.wait_ge(yc_done[k], i + 1)
                act.wait_ge(sel_ready[(k - 1) % LOTS], i + (1 if k == 0 else 2))
                nc.scalar.activation(off[:, :, :, :], rowb[:, k], ACT.Abs, scale=-1.0, bias=part[:, 0:1]
                                     ).then_inc(off_ready[k], 1)
                act.wait_ge(off_ready[k], i + 1)
                nc.scalar.activation(nodeT[:, k], off[:, :, 0, :], ACT.Relu, scale=-1.0, bias=ones[:, 0:1]
                                     ).then_inc(node_sel_ready[k], 1)
                nc.scalar.activation(relT[:, k], off[:, :, 1, :], ACT.Relu, scale=-1.0, bias=ones[:, 0:1]
                                     ).then_inc(sel_ready[k], 1)

            def body1(i, end):
                for k in range(LOTS):
                    act.wait_ge(mm_done[k], i + (C + 1))
                    for u in range(HB):
                        last = nc.scalar.activation(away[:, u, :], iota[:, :], ACT.Abs, scale=-1.0,
                                                    bias=tabs[:, DLOC, bass.ds(i * BODY + (k * HB + u), 1)])
                    last.then_inc(away_ready[k], 1)
                    act.wait_ge(away_ready[k], i + 1)
                    nc.scalar.activation(onehot[:, k], away[:, :, :], ACT.Relu, scale=-1.0, bias=ones[:, 0:1]
                                         ).then_inc(onehot_ready[k], 1)
                    if k + 3 < LOTS or not end:
                        selectors(i + (k + 3) // LOTS, (k + 3) % LOTS)
                    if k + 1 < LOTS or not end:
                        attention(i + (k + 1) // LOTS, (k + 1) % LOTS)
                    if k + 2 < LOTS or not end:
                        copy_yc(i + (k + 2) // LOTS, (k + 2) % LOTS)
                    act.wait_ge(gathered[1][k], i * 64 + 64)
                    act.wait_ge(onehot_ready[k], i + 1)
                    lot(i + 1, k)

            for k in range(3):
                selectors(0, k)
            copy_yc(0, 0)
            copy_yc(0, 1)
            attention(0, 0)
            with act.Fori(0, C - 1) as i:
                body1(i, False)
            body1(C - 1, True)
            norm(2)
            lots(2)
            transposes(2)
            norm(3)
            lots(3)
            transposes(3)

        @block.vector
        def _(dve):
            chain = [0]

            def step(ins):
                chain[0] += 1
                ins.then_inc(dve_chain, 1)
                dve.wait_ge(dve_chain, chain[0])

            tt, ts, cp = nc.vector.tensor_tensor, nc.vector.tensor_scalar, nc.vector.tensor_copy

            nc.vector.memset(nat[:, :, :], 0.0).then_inc(consts, 1)
            nc.vector.memset(wdiag[:, 1, :], 0.0).then_inc(consts, 1)
            nc.vector.memset(relc[:, :], 0.0).then_inc(consts, 1)
            nc.vector.memset(zeros[:, :], 0.0).then_inc(consts, 1)
            nc.vector.memset(ones[:, :], 1.0).then_inc(consts, 1)
            nc.vector.memset(padbf[:, 0:P], FAR).then_inc(consts, 1)
            nc.vector.memset(padbf[:, P:2 * P], 0.0).then_inc(consts, 1)
            nc.vector.memset(tcoli[:, 6:7], 0).then_inc(consts, 1)
            nc.vector.memset(tabs[:, 1:4, TILES + EXTRAS:STEPS], 0.0)
            nc.vector.memset(tabs[:, 0, TILES + EXTRAS:STEPS], FAR)
            free = [s[k] for s in (row_used, msg_ready, mm_done, sel_ready, yc_done, coef_ready) for k in range(LOTS)] + [yc_copied]
            for n, s in enumerate(free):
                nc.vector.memset(msg[:, 0, 0, n:n + 1], 0.0).then_inc(s, 1)
            dve.wait_ge(pads_set, 6)
            cp(iota[:, :], iota_i[:, :])
            step(cp(part[:, :], part_i[:, :]))
            step(nc.vector.tensor_scalar_add(part1[:, :], part[:, :], 1.0))
            step(ts(thr[:, :], iota[:, 0:EXTRAS], 1.0, float(P), ALU.add, ALU.mult))

            dve.wait_ge(edges_loaded, 15 * 16)
            dI, nI, sI, eI = (raw[:, a] for a in range(4))
            cp(rows[:, :, DLOC, :], dI)
            step(tt(rows[:, :, LAST, :], dI, nI, ALU.not_equal))
            step(cp(rows[:, :, ETY, :], eI))
            nc.vector.tensor_single_scalar(firstwi[:, 0, :], dI[:, :, 0], 7, ALU.arith_shift_right)
            step(nc.vector.tensor_single_scalar(nI, sI, P - 1, ALU.bitwise_and))
            step(nc.vector.tensor_single_scalar(eI, sI, 7, ALU.arith_shift_right))
            ins = nc.vector.scalar_tensor_tensor(rows[:, :, SRC, :], nI, float(BLOCKS), eI, ALU.mult, ALU.add)
            ins.then_inc(rows_ready, 1)
            step(cp(firstw[:, 0, :], firstwi[:, 0, :]))
            for c in range(ROWCH):
                last = ts(before[:, c, :], thr[:, :], rows[:, c, DLOC, P - 1:P], None, ALU.is_gt)
            last.then_inc(before_ready, 1)
            nc.vector.tensor_single_scalar(firstw[:, 1, :], firstw[:, 0, :], float(P), ALU.mult)
            step(nc.vector.tensor_single_scalar(firstwi[:, 1, :], firstw[:, 0, :], float(D), ALU.mult))
            tt(rloc[:, :, :], rows[:, :, DLOC, :], firstw[:, 1, :].unsqueeze(2).to_broadcast([P, ROWCH, P]), ALU.subtract)
            step(cp(rbf[:, :, 1, :], rows[:, :, ETY, :]))
            cp(rbf[:, :, 0, :], rloc[:, :, :]).then_inc(local_ready, 1)
            dve.wait_ge(count_done, 1)
            X = slice(0, EXTRAS)
            step(cp(tcol[X, 0:1], ps[X, 7 * BANK:7 * BANK + 1]))
            cp(tcoli[X, 0:1], tcol[X, 0:1])
            nc.vector.tensor_single_scalar(tcoli[X, 1:2], tcol[X, 0:1], 2.0, ALU.mult)
            step(ts(tcol[X, 1:2], tcol[X, 0:1], 2.0, 1.0, ALU.mult, ALU.add))
            nc.vector.tensor_single_scalar(tcoli[X, 2:3], tcol[X, 1:2], float(N_EDGES // HALF - 1), ALU.min
                                           ).then_inc(extra_ready, 1)

            dve.wait_ge(loaded, 38 * 16)
            step(nc.vector.tensor_scalar_add(opeps[:, :], opeps[:, :], 1.0))
            cp(wq[:, 0:MSG].rearrange("p (o b) -> p o b", o=D), wnat[:, :, :].rearrange("p b o -> p o b"))
            of = relc[:, :]
            for k in range(3):
                step(cp(relparts[:, k, :], of))
                if k < 2:
                    step(tt(relrest[:, k, :], of, relparts[:, k, :], ALU.subtract))
                    of = relrest[:, k, :]
            dve.wait_ge(wts_T, 1)
            cp(wdiag[:, 0, :], ps[:, 0:P])
            cp(wdiag[:, 2, :], ps[:, P:2 * P])
            cp(wq[:, MSG:MSG + 2 * D], ps[:, 2 * P:2 * P + 2 * D]).then_inc(wts_ready, 1)

            def norm(l):
                mean, var, std, r, a, b_ = (small[:, k] for k in range(6))
                wide = lambda v: v.unsqueeze(2).to_broadcast([P, BLOCKS, D])
                step(nc.vector.reduce_sum(mean, x[:, :, :], AX.X))
                step(nc.vector.tensor_single_scalar(mean, mean, 1.0 / D, ALU.mult))
                step(tt(h[:, :, :], x[:, :, :], wide(mean), ALU.subtract))
                step(tt(t[:, :, :], h[:, :, :], h[:, :, :], ALU.mult))
                step(nc.vector.reduce_sum(var, t[:, :, :], AX.X))
                ts(var, var, 1.0 / D, EPS, ALU.mult, ALU.add).then_inc(var_ready, 1)
                dve.wait_ge(std_ready, l + 1)
                step(nc.vector.reciprocal(r, std))
                step(tt(a, r, r, ALU.mult))
                step(tt(b_, a, var, ALU.mult))
                step(ts(a, b_, -0.5, 1.5, ALU.mult, ALU.add))
                step(tt(b_, a, r, ALU.mult))
                nc.vector.scalar_tensor_tensor(h[:, :, :], h[:, :, :], 0.0, wide(b_), ALU.max, ALU.mult
                                               ).then_inc(h_ready, 1)
                dve.wait_ge(h_ready, l + 1)

            norm(0)

            dve.wait_ge(extra_rows, 16)
            step(cp(tcoli[X, 3:4], xrow[X, DLOC, 0:1]))
            step(nc.vector.tensor_single_scalar(tcoli[X, 4:5], tcoli[X, 3:4], 7, ALU.arith_shift_right))
            step(cp(tcol[X, 4:5], tcoli[X, 4:5]))
            step(tt(tcol[X, 5:6], tcol[X, 4:5], part1[X, :], ALU.is_equal))
            nc.vector.tensor_single_scalar(tcoli[X, 5:6], part1[X, :], float(D), ALU.mult)
            step(nc.vector.tensor_single_scalar(tcol[X, 6:7], tcol[X, 5:6], FAR, ALU.mult))
            step(nc.vector.scalar_tensor_tensor(tcol[X, 7:8], part1[X, :], -float(P), tcol[X, 6:7], ALU.mult, ALU.add))
            step(ts(xloc[X, :], xrow[X, DLOC, :], tcol[X, 7:8], None, ALU.add))
            cp(xbf[X, 0, :], xloc[X, :])
            cp(xbf[X, 1, :], xrow[X, ETY, :]).then_inc(xlocal_ready, 1)
            dve.wait_ge(tabs_copied, ROWCH + 1)
            cp(srcT[:, STEPS:STEPS + BODY], tabs[:, SRC, 0:BODY])
            cp(srcT[:, 0:STEPS], tabs[:, SRC, :]).then_inc(tabs_ready, 1)

            def onehots(l, i, k):
                dve.wait_ge(mm_done[k], i + (l * C + 1))
                return tt(onehot[:, k], iota[:, :].unsqueeze(1).to_broadcast([P, HB, P]),
                          tabs[:, DLOC, bass.ds(i * BODY + k * HB, HB)].unsqueeze(2).to_broadcast([P, HB, P]),
                          ALU.is_equal)

            def per_edge(v, i, k, n):
                return tabs[:, v, bass.ds(i * BODY + k * HB, HB)].unsqueeze(2).to_broadcast([P, HB, n])

            with dve.Fori(0, C) as i:
                for k in range(LOTS):
                    dve.wait_ge(gathered[0][k], i * 64 + 64)
                    dve.wait_ge(attr_loaded[k], i * 16 + 16)
                    dve.wait_ge(mm_done[k], i + 1)
                    tt(total[:, k], grow[:, k], attr[:, k], ALU.add).then_inc(row_used[k], 1)
                    onehots(0, i, k)
                    dve.wait_ge(row_used[k], i + 2)
                    nc.vector.tensor_single_scalar(msg[:, k], total[:, k], 0.0, ALU.max).then_inc(msg_ready[k], 1)

            def residual(q, relu):
                xf = x[:, :, :].rearrange("p b f -> p (b f)")
                for b in range(BANKS):
                    w = slice(b * BANK, min((b + 1) * BANK, FEAT))
                    dve.wait_ge(lin_done, BANKS * q + b + 1)
                    if relu:
                        ins = nc.vector.scalar_tensor_tensor(xf[:, w], ps[:, w], 0.0, xf[:, w], ALU.max, ALU.add)
                    else:
                        ins = tt(xf[:, w], ps[:, w], xf[:, w], ALU.add)
                step(ins)

            tf, hf = (v[:, :, :].rearrange("p b f -> p (b f)") for v in (t, h))

            def scattered(l):
                for k in range(LOTS):
                    dve.wait_ge(mm_done[k], (l + 1) * C + 1)

            scattered(0)
            nc.vector.scalar_tensor_tensor(tf, hf, opeps[:, 0:1], acc, ALU.mult, ALU.add).then_inc(t_ready, 1)
            residual(0, False)
            norm(1)
            yf = y[:, :, :].rearrange("p b f -> p (b f)")
            for b in range(BLOCKS):
                at = (b % 4) * 2 * BANK + BANK
                dve.wait_ge(p1_done, b + 1)
                if b >= 16 and b % 4 == 0:
                    dve.wait_ge(p1_out[b // 4 % LOTS], 16 * (b // 16))
                cp(trow[:, b % 16, MSG // 2:MSG], ps[:, at:at + MSG // 2])
                at += MSG // 2
                tt(trow[:, b % 16, MSG:ROW1], ps[:, at:at + D], bias1[:, 0:D], ALU.add)
                tt(yf[:, b * D:(b + 1) * D], ps[:, at + D:at + 2 * D], bias1[:, D:2 * D], ALU.add).then_inc(p1_biased, 1)

            def score_terms(i, k, n):
                dve.wait_ge(gathered[1][k], i * 64 + 64)
                dve.wait_ge(yc_copied, n + 2)
                tt(yprod[:, :, :], g1[:, k, :, MSG:ROW1], yc[:, k, :, BASES:YC], ALU.mult).then_inc(yprod_ready[k], 1)

            def score_sum(i, k):
                dve.wait_ge(yprod_ready[k], i + 1)
                nc.vector.reduce_sum(score[:, k], yprod[:, :, :], AX.X).then_inc(score_ready[k], 1)

            def body1(i, end):
                for k in range(LOTS):
                    dve.wait_ge(att_ready[k], i + 1)
                    cp(coef[:, :, BASES:BAS1], tabs[:, LAST, bass.ds(i * BODY + k * HB, HB)].unsqueeze(2))
                    tt(coef[:, :, 0:BASES], yc[:, k, :, 0:BASES], att[:, k].unsqueeze(2).to_broadcast([P, HB, BASES]),
                       ALU.mult).then_inc(coef_ready[k], 1)
                    ahead = (i + (k + 1) // LOTS, (k + 1) % LOTS) if k + 1 < LOTS or not end else None
                    if ahead:
                        score_terms(*ahead, i * LOTS + (k + 1))
                    dve.wait_ge(coef_ready[k], i + 2)
                    dve.wait_ge(msg_ready[(k - 1) % LOTS], i + (C + (1 if k == 0 else 2)))
                    tt(prod[:, :, :, :], g1[:, k, :, 0:MSG].rearrange("p u (o b) -> p u o b", o=D),
                       coef[:, :, :].unsqueeze(2).to_broadcast([P, HB, D, BAS1]), ALU.mult).then_inc(row_used[k], 1)
                    if ahead:
                        score_sum(*ahead)
                    dve.wait_ge(row_used[k], i + (C + 2))
                    dve.wait_ge(mm_done[k], i + (C + 1))
                    nc.vector.reduce_sum(msg[:, k], prod[:, :, :, :], AX.X).then_inc(msg_ready[k], 1)

            score_terms(0, 0, 0)
            score_sum(0, 0)
            with dve.Fori(0, C - 1) as i:
                body1(i, False)
            body1(C - 1, True)
            scattered(1)
            step(nc.vector.scalar_tensor_tensor(x[:, :, :].rearrange("p b f -> p (b f)"), acc, 0.0,
                                                x[:, :, :].rearrange("p b f -> p (b f)"), ALU.max, ALU.add))
            norm(2)

            with dve.Fori(0, C) as i:
                for k in range(LOTS):
                    onehots(2, i, k)
                    dve.wait_ge(gathered[2][k], i * 64 + 64)
                    tt(msg[:, k], grow[:, k], per_edge(WGT, i, k, D), ALU.mult).then_inc(msg_ready[k], 1)
            scattered(2)
            cp(tf, acc).then_inc(t_ready, 1)
            residual(1, True)
            norm(3)

            with dve.Fori(0, C) as i:
                for k in range(LOTS):
                    onehots(3, i, k).then_inc(msg_ready[k], 1)
            scattered(3)
            cp(tf, acc).then_inc(t_ready, 1)
            residual(2, False)
            nc.vector.tensor_copy(total[:, 0, 0, 0:1], x[:, 0, 0:1]).then_inc(h_ready, 1)

        @block.tensor
        def _(pe):
            mm = nc.tensor.matmul
            pe.wait_ge(consts, 8)
            pe.wait_ge(ident_ready, 2)
            pe.wait_ge(before_ready, 1)
            for c in range(ROWCH):
                last = mm(ps[0:EXTRAS, 7 * BANK:7 * BANK + 1], before[:, c, :], ones[:, 0:1], start=(c == 0),
                          stop=(c == ROWCH - 1))
            last.then_inc(count_done, 1)
            pe.wait_ge(loaded, 38 * 16)
            nc.tensor.transpose(ps[:, 0:P], nat[:, 0, :], ident[:, :])
            nc.tensor.transpose(ps[:, P:2 * P], nat[:, 1, :], ident[:, :])
            nc.tensor.transpose(ps[:, 2 * P:2 * P + D], anat[:, 0].rearrange("o r i -> o (r i)"), ident[0:D, 0:D])
            nc.tensor.transpose(ps[:, 2 * P + D:2 * P + 2 * D], anat[:, 1].rearrange("o r i -> o (r i)"),
                                ident[0:D, 0:D]).then_inc(wts_T, 1)
            pe.wait_ge(wts_ready, 1)

            pe.wait_ge(local_ready, 1)
            for c in range(ROWCH + 1):
                n = P if c < FULL_CH else TILES - FULL_CH * P if c == FULL_CH else EXTRAS
                if c > FULL_CH:
                    pe.wait_ge(xlocal_ready, 1)
                if c >= 7:
                    pe.wait_ge(tabs_copied, c - 6)
                for a in range(4):
                    of = (xloc[0:n, :] if c > FULL_CH else rloc[0:n, c, :]) if a == DLOC else \
                        xrow[0:n, a, :] if c > FULL_CH else rows[0:n, c, a, :]
                    at = (c % 7) * BANK + a * P
                    last = nc.tensor.transpose(ps[:, at:at + n], of, ident[0:n, 0:n])
                last.then_inc(tabs_T, 1)
            pe.wait_ge(tabs_copied, ROWCH + 1)
            pe.wait_ge(window_loaded, 16)

            def clear():
                for b in range(BANKS):
                    mm(ps[:, b * BANK:(b + 1) * BANK], zeros[0:1, 0:P], zeros[0:1, :], start=True, stop=True,
                       skip_group_check=True)

            def windows(i, n):
                _, w = nc.values_load_multi_w_load_instructions(
                    window[0:1, bass.ds(i * BODY, n)], engines=(mybir.EngineType.PE,), min_val=0,
                    max_val=(BLOCKS - 1) * D, skip_runtime_bounds_check_because="windows of nodes below N_NODES")
                return w

            def scatter(l, i, k, w, of):
                pe.wait_ge(msg_ready[k], i + (l * C + 2))
                for u in range(HB):
                    last = mm(ps[:, bass.ds(w[u], D)], onehot[:, k, u, :], of[:, k, u, :], start=False, stop=True,
                              skip_group_check=True)
                last.then_inc(mm_done[k], 1)

            def transposes(of):
                for b in range(BANKS):
                    for g in range(4 * b, min(4 * b + 4, GROUPS)):
                        n = min(P, FEAT - g * P)
                        last = nc.tensor.transpose(ps[0:n, g * P:(g + 1) * P], of[:, g * P:g * P + n], ident[:, :])
                    last.then_inc(hT_done, 1)

            tf, hf = (v[:, :, :].rearrange("p b f -> p (b f)") for v in (t, h))

            def linear(q, copies, w, bias):
                pe.wait_ge(t_ready, q + 1)
                transposes(tf)
                for b in range(BANKS):
                    n = min(BANK, FEAT - b * BANK)
                    pe.wait_ge(hT_copied, BANKS * (copies + 1) if b == 0 else BANKS * copies + b + 1)
                    mm(ps[:, b * BANK:b * BANK + n], ones[0:1, :], biasrow[:, bias, 0:n], start=True, stop=False,
                       skip_group_check=True)
                    for g in range(4 * b, min(4 * b + 4, GROUPS)):
                        m = min(P, FEAT - g * P)
                        last = mm(ps[:, g * P:g * P + m], tT[0:m, g * P:(g + 1) * P], wdiag[0:m, w, 0:m],
                                  start=False, stop=True, skip_group_check=True)
                    last.then_inc(lin_done, 1)

            clear()
            with pe.Fori(0, C) as i:
                w = windows(i, BODY)
                for k in range(LOTS):
                    scatter(0, i, k, w[k * HB:], msg)
            linear(0, 0, 0, 0)

            pe.wait_ge(h_ready, 2)
            pe.wait_ge(lin_done, BANKS)
            transposes(hf)
            pe.wait_ge(hT_copied, 2 * BANKS)
            for g in range(GROUPS):
                four = range(4 * g, min(4 * g + 4, BLOCKS))
                if g:
                    pe.wait_ge(p1_copied, 4 * g)
                    pe.wait_ge(p1_biased, 4 * g)

                def operands(b):
                    q, at = slice((b % 4) * D, (b % 4 + 1) * D), (b % 4) * 2 * BANK
                    return q, tT[q, g * P:(g + 1) * P], ps[:, at:at + MSG // 2], \
                        ps[:, at + BANK:at + BANK + MSG // 2 + 2 * D]

                for b in four:
                    q, lhsT, one, _ = operands(b)
                    mm(one, lhsT, wq[q, 0:MSG // 2], start=True, stop=True)
                for b in four:
                    q, lhsT, _, two = operands(b)
                    mm(two, lhsT, wq[q, MSG // 2:MSG + 2 * D], start=True, stop=True).then_inc(p1_done, 1)
            pe.wait_ge(p1_copied, BLOCKS)
            pe.wait_ge(p1_biased, BLOCKS)
            clear()

            def edge_terms(i, k, w, n):
                pe.wait_ge(node_sel_ready[k], i + 1)
                pe.wait_ge(sel_ready[k], i + 2)
                pe.wait_ge(yc_copied, n)
                for u in range(HB):
                    for part_ in range(3):
                        mm(ps7[:, u, :], relT[:, k, u, :], relparts[:, part_, :], start=(part_ == 0), stop=False,
                           skip_group_check=True)
                    last = mm(ps7[:, u, BASES:YC], nodeT[:, k, u, :], yf[:, bass.ds(w[u], D)], start=False, stop=True,
                              skip_group_check=True)
                last.then_inc(yc_done[k], 1)

            yf = tf
            def body1(i, end):
                w = windows(i, BODY if end else BODY + 2 * HB)
                for k in range(LOTS):
                    if k + 2 < LOTS or not end:
                        edge_terms(i + (k + 2) // LOTS, (k + 2) % LOTS, w[(k + 2) * HB:], i * LOTS + (k + 3))
                    pe.wait_ge(onehot_ready[k], i + 1)
                    scatter(1, i, k, w[k * HB:], msg)

            w = windows(0, 2 * HB)
            edge_terms(0, 0, w, 1)
            edge_terms(0, 1, w[HB:], 2)
            with pe.Fori(0, C - 1) as i:
                body1(i, False)
            body1(C - 1, True)
            pe.wait_ge(h_ready, 3)
            clear()
            with pe.Fori(0, C) as i:
                w = windows(i, BODY)
                for k in range(LOTS):
                    scatter(2, i, k, w[k * HB:], msg)
            linear(1, 2, 1, 1)
            pe.wait_ge(h_ready, 4)
            clear()
            with pe.Fori(0, C) as i:
                w = windows(i, BODY)
                for k in range(LOTS):
                    pe.wait_ge(gathered[3][k], i * 64 + 64)
                    scatter(3, i, k, w[k * HB:], grow)
            linear(2, 3, 2, 2)


_INS = ['x', 'src', 'dst', 'edge_attr_32', 'edge_type_86', 'edge_weight', 'L0_gnn_W', 'L0_gnn_b', 'L0_gnn_eps',
        'L1_gnn_weight', 'L1_gnn_w_comp', 'L1_gnn_self_loop_weight', 'L1_gnn_A1_w', 'L1_gnn_A1_b', 'L1_gnn_A2_w',
        'L1_gnn_A2_b', 'L1_gnn_rel_emb', 'L2_gnn_W', 'L2_gnn_b', 'L3_gnn_W', 'L3_gnn_b']


def kernel(**inputs):
    import numpy as _np
    import concourse.bacc as _bacc
    from concourse import mybir as _mybir
    from concourse.bass_utils import run_bass_kernel_spmd as _run

    nc = _bacc.Bacc("TRN2", target_bir_lowering=False, num_devices=1)
    arrays, args = {}, []
    for name in _INS:
        a = _np.ascontiguousarray(inputs[name])
        arrays[f"in_{name}"] = a
        args.append(nc.dram_tensor(f"in_{name}", a.shape, _mybir.dt.from_np(a.dtype), kind="ExternalInput").ap())
    out = nc.dram_tensor("out_nodes", (N_NODES, D), F32, kind="ExternalOutput").ap()
    gnn(nc, *args, out)
    r = _run(nc, [arrays], core_ids=[0])
    return r.results[0]["out_nodes"]
```

```python
import concourse.bass as bass
from concourse import mybir
from contextlib import ExitStack

F32 = mybir.dt.float32
I32 = mybir.dt.int32
BF16 = mybir.dt.bfloat16
ALU = mybir.AluOpType
ACT = mybir.ActivationFunctionType
AX = mybir.AxisListType

P = 128
N_NODES, N_EDGES, D = 12500, 200000, 32
RELS, BASES = 86, 16
EPS = 1e-5

BLOCKS = -(-N_NODES // P)
LAST_NODES = N_NODES - (BLOCKS - 1) * P
TILES = -(-N_EDGES // P)
ROWCH = -(-TILES // P)
FULL_CH = TILES // P
TAIL_TILES = N_EDGES // P - FULL_CH * P
HALF = N_EDGES - (N_EDGES // P) * P
WB = 8
EXN = BLOCKS - 1
EXW = -(-BLOCKS // WB) - 1
EXTRAS = EXN + EXW
LOTS, HB = 4, 4
BODY = LOTS * HB
STEPS_N = -(-(EXN + TILES) // BODY) * BODY
STEPS_W = -(-(TILES + EXW) // BODY) * BODY
FIRST = (EXN, 0, EXN, EXN)
COLS = EXN + STEPS_W
XW = EXN + TILES
LAST_LOTS = -(-((TILES + EXW - 1) % BODY + 1) // HB)
C = tuple(n // BODY for n in (STEPS_W, STEPS_N, STEPS_W, STEPS_W))
BEFORE = tuple(sum(C[:l]) for l in range(5))
MAIN = (N_EDGES // P) // BODY
TAIL = STEPS_W - MAIN * BODY
P1_LOTS = -(-BLOCKS // 4)
FAR = float(1 << 20)
FEAT = BLOCKS * D
BANK = 512
GROUPS = -(-BLOCKS // 4)
BANKS = -(-FEAT // BANK)
BLOCKS_IN = BANK // D
MSG = D * BASES
ROW1 = MSG + D
PROD = MSG + 3 * D
WINW = -(-BLOCKS // WB)
ID0, ID = WINW * WB * D, 2 * WB
ORDER = (0, 1, 2, 0, 1)
PASSES = ((0, (0, 0, 0, 1)), (1, (1, 1, 2, 2)))
AHEAD = 2
YC = BASES + D


def gnn(nc, x_in, src, dst, edge_attr, etype, weight, W0, b0, eps0, W1, wcomp, wself, A1, A1b, A2, A2b,
        relemb, W2, b2, W3, b3, out):
    tableD = [nc.dram_tensor(f"table{l}", (BLOCKS * P, ROW1 if l == 1 else D), F32, kind="Internal").ap()
              for l in range(4)]
    selfD = nc.dram_tensor("self_loop_table", (BLOCKS * P, D), F32, kind="Internal").ap()
    rowsD = nc.dram_tensor("edge_rows", (ROWCH * P, 4 * P), F32, kind="Internal").ap()
    stepsD = nc.dram_tensor("step_rows", (STEPS_N, 2 * P), BF16, kind="Internal").ap()
    windowN = nc.dram_tensor("step_window_narrow", (STEPS_N, 1), I32, kind="Internal").ap()
    windowW = nc.dram_tensor("step_window_wide", (STEPS_W, 1), I32, kind="Internal").ap()
    attrD = nc.dram_tensor("attr_tail", (TAIL * P, D), F32, kind="Internal").ap()

    ctx = ExitStack()
    with ctx:
        ctx.enter_context(nc.allow_non_contiguous_dma("small weights and window offsets"))

        def sb(name, shape, dt=F32):
            return ctx.enter_context(nc.sbuf_tensor(name, shape, dt))

        def sem(name):
            return ctx.enter_context(nc.semaphore(name))

        def lotwise(name):
            return [sem(f"{name}_{h}") for h in range(LOTS)]

        def pairwise(name):
            return [sem(f"{name}_{p}") for p in range(LOTS // 2)]

        def pair(p, v):
            return v[:, 2 * p:2 * p + 2].rearrange("p h u f -> p (h u) f")

        x = sb("x", [P, BLOCKS, D])
        h = sb("h", [P, BLOCKS, D])
        t = sb("t", [P, BLOCKS, D])
        tT = sb("tT", [P, GROUPS * P])
        tabs = sb("tabs", [P, 4, COLS])
        DLOC, BLK, WGT, SRC = range(4)
        srcT = tabs[:, SRC, :].bitcast(I32)
        node = sb("node", [P, COLS], BF16)
        lastT = sb("last", [P, 2, COLS], BF16)
        lastrow = sb("lastrow", [P, LOTS, HB, 2, WB], BF16)
        selfv = sb("selfv", [P, WINW * WB])
        has_edge = sb("has_edge", [P, WINW * WB])
        selfi = sb("selfi", [P, WINW * WB], I32)
        selfidx = sb("selfidx", [P, 1], I32)
        selfrow = sb("selfrow", [P, D])
        RSRC, DST, RWGT, ETY = range(4)
        window = sb("window", [1, STEPS_N], I32)
        onehot = sb("onehot", [P, LOTS, HB, P])
        msg = sb("msg", [P, LOTS, HB, D])
        attr = sb("attr", [P, LOTS, HB, D])
        grow = sb("grow", [P, LOTS, HB, D])
        total = sb("total", [P, LOTS, HB, D])
        idx = sb("idx", [P, LOTS, HB], I32)
        iota_i = sb("iota_i", [P, P], I32)
        iota = sb("iota", [P, P])
        iotab = sb("iotab", [P, P], BF16)
        mask = sb("mask", [P, LOTS, HB, WB])
        wmask = sb("wmask", [P, LOTS, HB, WB])
        part_i = sb("part_i", [P, 1], I32)
        part = sb("part", [P, 1])
        part1 = sb("part1", [P, 1])
        thr = sb("thr", [P, EXTRAS])
        ident = sb("ident", [P, P])
        identb = sb("identb", [P, P], BF16)
        zeros = sb("zeros", [1, BANK])
        ones = sb("ones", [P, P])
        nat = sb("nat", [P, 2, P])
        wdiag = sb("wdiag", [P, 3, P])
        anat = sb("anat", [D, 2, 4, D])
        wq = sb("wq", [P, PROD])
        wparts = sb("wparts", [P, 2, PROD], BF16)
        biasrow = sb("biasrow", [1, 3, D])
        bias1 = sb("bias1", [P, 2 * D])
        relc = sb("relc", [P, YC])
        relparts = sb("relparts", [P, 3, YC], BF16)
        relrest = sb("relrest", [P, 2, YC])
        unused = sb("unused", [1, 4, LOTS, 4])
        opeps = sb("opeps", [P, 1])
        small = sb("small", [P, 6, BLOCKS])
        arena = sb("arena", [P, 19600])

        used = [0]

        def region(n, dt=F32):
            a = arena[:, used[0]:used[0] + n]
            used[0] += n
            return a if dt == F32 else a.bitcast(dt)

        raw = region(4 * ROWCH * P, I32).rearrange("p (a c e) -> p a c e", a=4, c=ROWCH)
        rows = region(ROWCH * 4 * P).rearrange("p (c a e) -> p c a e", c=ROWCH, a=4)
        rloc = region(ROWCH * P).rearrange("p (c e) -> p c e", c=ROWCH)
        wloc = region(ROWCH * P).rearrange("p (c e) -> p c e", c=ROWCH)
        rbf = region(ROWCH * P, BF16).rearrange("p (c a e) -> p c a e", c=ROWCH, a=2)
        xrow = region(4 * P).rearrange("p (a e) -> p a e", a=4)
        xattr = arena[:, 0:P * D]
        xloc = region(P)
        xbf = region(P, BF16).rearrange("p (a e) -> p a e", a=2)
        padbf = region(P, BF16)
        tcol = region(16)
        tcoli = region(16, I32)
        firstw = region(4 * ROWCH).rearrange("p (a c) -> p a c", a=4)
        firstwi = region(4 * ROWCH, I32).rearrange("p (a c) -> p a c", a=4)
        tmpi = arena[:, P * D:P * D + 2 * COLS].bitcast(I32).rearrange("p (a s) -> p a s", a=2)
        before = tT[:, 0:ROWCH * EXTRAS].rearrange("p (c w) -> p c w", c=ROWCH)
        wnat = tT[:, ROWCH * EXTRAS:ROWCH * EXTRAS + (BASES + 1) * D].rearrange("p (b o) -> p b o", b=BASES + 1)
        tflat = t[:, :, :].rearrange("p b f -> p (b f)")
        wrest, wsplit = tflat[:, 0:PROD], tflat[:, PROD:4 * PROD].bitcast(BF16)[:, 0:3 * PROD].rearrange(
            "p (a f) -> p a f", a=3)
        used[0] = 0
        wmsg = arena[:, P * D:P * D + BODY * WB * D].rearrange("p (h u w f) -> p h u w f", h=LOTS, u=HB, w=WB)
        onehotb = arena[:, P * D + BODY * WB * D:P * D + BODY * (WB * D + P // 2)].bitcast(BF16).rearrange(
            "p (h u n) -> p h u n", h=LOTS, u=HB)
        g1 = region(LOTS * HB * ROW1).rearrange("p (h u f) -> p h u f", h=LOTS, u=HB)
        prods = [v.rearrange("p (u o b) -> p u o b", u=HB, o=D) for v in (region(HB * MSG), tT[:, 0:HB * MSG])]
        rowb = region(LOTS * HB * P, BF16).rearrange("p (h u a e) -> p h u a e", h=LOTS, u=HB, a=2)
        nodeT = region(LOTS * HB * P).rearrange("p (h u e) -> p h u e", h=LOTS, u=HB)
        relT = region(LOTS * HB * P // 2, BF16).rearrange("p (h u e) -> p h u e", h=LOTS, u=HB)
        off = region(HB * 2 * P).rearrange("p (u a e) -> p u a e", u=HB, a=2)
        yc = region(LOTS * HB * YC).rearrange("p (h u f) -> p h u f", h=LOTS, u=HB)
        yprod = region(2 * HB * D).rearrange("p (u f) -> p u f", f=D)
        coef = region(LOTS * HB * BASES).rearrange("p (h u b) -> p h u b", h=LOTS, u=HB)
        score = region(LOTS * HB)
        att = region(LOTS * HB)
        away = region(HB * P).rearrange("p (u n) -> p u n", u=HB)
        assert used[0] <= 19600, used[0]
        trow = arena[:, 0:16 * ROW1].rearrange("p (r f) -> p r f", r=16)
        hparts = arena[:, 16 * ROW1:16 * ROW1 + BLOCKS * len(ORDER) * D // 2].bitcast(BF16).rearrange(
            "p (b a f) -> p b a f", b=BLOCKS, a=len(ORDER))
        partsT = tT[:, 0:6 * BANK].bitcast(BF16).rearrange("p (r b a n) -> p r b a n", r=6, b=4, a=2)
        y = t

        ps = ctx.enter_context(nc.psum_tensor("ps", [P, 8 * BANK], F32))
        acc = ps[:, 0:FEAT]
        W7 = 7 * BANK
        ps7 = ps[:, 7 * BANK:7 * BANK + HB * YC].rearrange("p (u f) -> p u f", u=HB)

        def parts_bank(g):
            at = (6 + g % 2) * BANK
            return ps[:, at:at + BANK].bitcast(BF16).rearrange("p (b a n) -> p b a n", b=4, a=2)

        def after(i, k, n, end):
            return None if end and k + n >= LOTS else (i + (k + n) // LOTS, (k + n) % LOTS)

        x_loaded = sem("x_loaded")
        loaded = sem("weights_loaded")
        ends_loaded = sem("edge_ends_loaded")
        kinds_loaded = sem("edge_kinds_loaded")
        rows_cast = sem("rows_cast")
        pads_set = sem("pads_set")
        consts = sem("consts_ready")
        ident_ready = sem("identity_ready")
        dve_chain = sem("dve_chain")
        wts_T = sem("weights_transposed")
        wts_ready = sem("weights_ready")
        rows_ready = sem("rows_ready")
        src_T = sem("sources_transposed")
        src_copied = sem("sources_copied")
        rows_out = sem("rows_written")
        before_ready = sem("before_ready")
        count_done = sem("extra_tiles_counted")
        extra_ready = sem("extra_tiles_ready")
        extra_rows = sem("extra_rows_gathered")
        extra_attr = sem("extra_attr_gathered")
        local_ready = sem("local_nodes_ready")
        xlocal_ready = sem("extra_local_ready")
        tabs_T = sem("tables_transposed")
        tabs_copied = sem("tables_copied")
        tabs_ready = sem("tables_ready")
        steps_out = sem("steps_written")
        window_loaded = sem("window_loaded")
        tail_ready = sem("attr_tail_written")
        added = sem("residual_added")
        mean_ready = sem("mean_ready")
        centered = sem("centered")
        squared = sem("squared")
        var_ready = sem("variance_ready")
        std_ready = sem("std_ready")
        h_ready = sem("h_ready")
        table_out = [sem(f"table_written_{l}") for l in range(4)]
        hT_done = sem("transposed")
        hT_copied = sem("transposes_copied")
        lin_done = sem("linear_done")
        t_ready = sem("t_ready")
        acc_free = sem("sums_read")
        idx_ready = lotwise("idx_ready")
        gathered = [lotwise(f"gathered{l}") for l in range(4)]
        row_used = lotwise("gathered_used")
        attr_loaded = lotwise("attr_loaded")
        masked = lotwise("mask_ready")
        weighted = lotwise("weighted_mask_ready")
        msg_ready = lotwise("msg_ready")
        mm_done = lotwise("scatter_done")
        high_ready = sem("high_parts_ready")
        rest_ready = sem("rests_ready")
        mid_ready = sem("middle_parts_ready")
        parts_ready = sem("parts_ready")
        partsT_done = sem("parts_transposed")
        partsT_copied = sem("transposed_parts_copied")
        p1_done = sem("node_products_done")
        p1_copied = sem("node_products_copied")
        p1_biased = sem("node_products_copied_by_vector")
        self_out = sem("self_loop_table_written")
        self_found = sem("last_rows_found")
        self_idx_ready = sem("self_idx_ready")
        self_gathered = sem("self_gathered")
        self_used = sem("self_used")
        p1_out = lotwise("node_products_written")
        steps_loaded = lotwise("step_rows_loaded")
        sel_ready = lotwise("selectors_ready")
        yc_done = lotwise("yc_done")
        yc_copied = sem("yc_copied")
        yprod_ready = pairwise("yprod_ready")
        score_ready = pairwise("score_ready")
        away_ready = lotwise("distance_ready")
        off_ready = lotwise("selector_distance_ready")
        node_sel_ready = lotwise("node_selector_ready")
        onehot_ready = lotwise("onehot_ready")
        att_ready = pairwise("attention_ready")
        coef_ready = pairwise("coef_ready")
        stored = sem("output_stored")

        block = ctx.enter_context(nc.Block())

        @block.sync
        def _(sp):
            n_full = FULL_CH * P * P
            n_tail = n_full + TAIL_TILES * P
            nb = BLOCKS - 1
            sp.dma_start(x[:, 0:nb, :], x_in[0:nb * P, :].rearrange("(b p) f -> p b f", p=P)).then_inc(x_loaded, 16)
            sp.wait_ge(pads_set, 4)
            sp.dma_start(x[0:LAST_NODES, nb, :], x_in[nb * P:N_NODES, :]).then_inc(x_loaded, 16)

            def edge_rows(to, of, shift, there):
                sp.dma_start(to[:, 0:FULL_CH, :], of[shift:n_full + shift].rearrange("(c p e) -> p c e", p=P, e=P)
                             ).then_inc(there, 16)
                sp.dma_start(to[0:TAIL_TILES, FULL_CH, :],
                             of[n_full + shift:n_tail + shift].rearrange("(p e) -> p e", e=P)
                             ).then_inc(there, 16)
                sp.dma_start(to[TAIL_TILES:TAIL_TILES + 1, FULL_CH, 0:HALF - shift],
                             of[n_tail + shift:N_EDGES].rearrange("(a e) -> a e", a=1)).then_inc(there, 16)

            edge_rows(raw[:, 0], dst, 0, ends_loaded)
            edge_rows(raw[:, 1], dst, 1, ends_loaded)
            edge_rows(raw[:, 2], src, 0, ends_loaded)
            edge_rows(raw[:, 3], etype, 0, kinds_loaded)
            edge_rows(rows[:, :, RWGT, :], weight, 0, kinds_loaded)
            sp.dma_start(attrD[0:N_EDGES - MAIN * BODY * P, :], edge_attr[MAIN * BODY * P:N_EDGES, :]
                         ).then_inc(tail_ready, 16)
            at = N_EDGES - MAIN * BODY * P
            sp.dma_start(attrD[at:at + P - HALF, :], edge_attr[0:P - HALF, :]).then_inc(tail_ready, 16)
            x0 = at + P - HALF
            x1 = x0 + EXW * P
            sp.dma_start(attrD[x1:TAIL * P, :], edge_attr[0:TAIL * P - x1, :]).then_inc(tail_ready, 16)

            def put_table(l):
                for b in range(BANKS):
                    sp.wait_ge(h_ready, BANKS * l + b + 1)
                    w = slice(b * BLOCKS_IN, min((b + 1) * BLOCKS_IN, BLOCKS))
                    sp.dma_start(tableD[l].rearrange("(p b) f -> p b f", p=P)[:, w, :], h[:, w, :]
                                 ).then_inc(table_out[l], 16)

            by_tile = rowsD.rearrange("(c p) (a e) -> p c a e", p=P, a=4)
            sp.wait_ge(rows_cast, 2)
            sp.wait_ge(kinds_loaded, 6 * 16)
            sp.dma_start(by_tile[:, :, DST:, :], rows[:, :, DST:, :]).then_inc(rows_out, 16)
            put_table(0)
            sp.wait_ge(rows_ready, 1)
            sp.dma_start(by_tile[:, :, RSRC, :], rows[:, :, RSRC, :]).then_inc(rows_out, 16)
            sp.wait_ge(local_ready, 2)
            st = stepsD.rearrange("s (a e) -> s a e", a=2)
            rest = TILES - FULL_CH * P
            sp.dma_start(st[EXN:EXN + FULL_CH * P].rearrange("(c p) a e -> p c a e", p=P), rbf[:, 0:FULL_CH]
                         ).then_inc(steps_out, 16)
            sp.dma_start(st[EXN + FULL_CH * P:EXN + TILES], rbf[0:rest, FULL_CH]).then_inc(steps_out, 16)
            for windowD, at, a in ((windowN, EXN, 1), (windowW, 0, 3)):
                sp.dma_start(windowD[at:at + FULL_CH * P].rearrange("(c p) a -> p (c a)", p=P),
                             firstwi[:, a, 0:FULL_CH]).then_inc(steps_out, 16)
                sp.dma_start(windowD[at + FULL_CH * P:at + TILES], firstwi[0:rest, a, FULL_CH:ROWCH]
                             ).then_inc(steps_out, 16)
            sp.wait_ge(xlocal_ready, 1)
            sp.dma_start(st[0:EXN], xbf[EXW:EXTRAS]).then_inc(steps_out, 16)
            sp.dma_start(windowN[0:EXN], tcoli[EXW:EXTRAS, 5:6]).then_inc(steps_out, 16)
            sp.dma_start(windowW[TILES:TILES + EXW], tcoli[0:EXW, 5:6]).then_inc(steps_out, 16)
            pads_n, pads_w = STEPS_N - EXN - TILES, STEPS_W - TILES - EXW
            sp.dma_start(stepsD[EXN + TILES:STEPS_N], padbf[0:pads_n]).then_inc(steps_out, 16)
            sp.dma_start(windowN[EXN + TILES:STEPS_N], tcoli[0:pads_n, 6:7]).then_inc(steps_out, 16)
            sp.dma_start(windowW[TILES + EXW:STEPS_W], tcoli[0:pads_w, 6:7]).then_inc(steps_out, 16)
            sp.wait_ge(steps_out, 12 * 16)

            def put_windows(of):
                sp.dma_start(window[:, 0:of.shape[0]], of.rearrange("s a -> a s")).then_inc(window_loaded, 16)

            put_windows(windowW)
            sp.wait_ge(extra_attr, 32)
            sp.dma_start(attrD[x0:x1, :].rearrange("(w e) f -> w (e f)", e=P), xattr[0:EXW, :]
                         ).then_inc(tail_ready, 16)

            with sp.Fori(0, MAIN) as i:
                for k in range(LOTS):
                    sp.wait_ge(row_used[k], i + 1)
                    sp.dma_start(attr[:, k], edge_attr[bass.ds(i * (BODY * P) + k * (HB * P), HB * P), :]
                                 .rearrange("(u p) f -> p u f", p=P)).then_inc(attr_loaded[k], 16)
            sp.wait_ge(tail_ready, 4 * 16)
            with sp.Fori(0, C[0] - MAIN) as i:
                for k in range(LOTS):
                    sp.wait_ge(row_used[k], i + (MAIN + 1))
                    sp.dma_start(attr[:, k], attrD[bass.ds(i * (BODY * P) + k * (HB * P), HB * P), :]
                                 .rearrange("(u p) f -> p u f", p=P)).then_inc(attr_loaded[k], 16)

            sp.wait_ge(h_ready, 2 * BANKS)
            put_windows(windowN)
            t1 = tableD[1].rearrange("(p b) f -> p b f", p=P)
            for m in range(P1_LOTS):
                b, e = 4 * m, min(4 * m + 4, BLOCKS)
                sp.wait_ge(p1_copied, e)
                sp.wait_ge(p1_biased, e)
                sp.dma_start(t1[:, b:e, :], trow[:, b % 16:b % 16 + e - b, :]).then_inc(p1_out[m % LOTS], 16)
                if e % BLOCKS_IN == 0 or e == BLOCKS:
                    w = slice((e - 1) // BLOCKS_IN * BLOCKS_IN, e)
                    sp.dma_start(selfD.rearrange("(p b) f -> p b f", p=P)[:, w, :], h[:, w, :]).then_inc(self_out, 16)

            with sp.Fori(0, C[1]) as i:
                for k in range(LOTS):
                    sp.wait_ge(sel_ready[k], i + 1)
                    sp.dma_start(rowb[:, k].rearrange("p u a e -> p (u a e)"),
                                 stepsD[bass.ds(i * BODY + k * HB, HB), :].rearrange("s f -> (s f)")
                                 .partition_broadcast(P)).then_inc(steps_loaded[k], 16)

            put_table(2)
            put_windows(windowW)
            put_table(3)
            for b in range(BANKS):
                sp.wait_ge(added, 4 * BANKS + b + 1)
                w0, w1 = b * BLOCKS_IN, min((b + 1) * BLOCKS_IN, BLOCKS - 1)
                sp.dma_start(out[w0 * P:w1 * P, :].rearrange("(b p) f -> p b f", p=P), x[:, w0:w1, :]
                             ).then_inc(stored, 16)
            sp.dma_start(out[w1 * P:N_NODES, :], x[0:LAST_NODES, w1, :]).then_inc(stored, 16)
            sp.wait_ge(stored, (BANKS + 1) * 16)

        @block.gpsimd
        def _(pool):
            last = slice(FULL_CH, ROWCH)
            pool.memset(raw[:, 0:2, last, :], int(FAR)).then_inc(pads_set, 1)
            pool.memset(raw[:, 2:4, last, :], 0).then_inc(pads_set, 1)
            pool.memset(rows[:, last, RWGT, :], 0.0).then_inc(pads_set, 1)
            pool.memset(x[:, BLOCKS - 1, :], 0.0).then_inc(pads_set, 1)
            pool.iota(iota_i[:, :], pattern=[[1, P]], base=0, channel_multiplier=0).then_inc(pads_set, 1)
            pool.iota(part_i[:, :], pattern=[[0, 1]], base=0, channel_multiplier=1).then_inc(pads_set, 1)
            pool.memset(ident[:, :], 0.0).then_inc(ident_ready, 1)
            pool.wait_ge(ident_ready, 1)
            pool.affine_select(out=ident[:, :], in_=ident[:, :], compare_op=ALU.not_equal, fill=1.0, base=0,
                               pattern=[[-1, P]], channel_multiplier=1).then_inc(ident_ready, 1)

            pool.wait_ge(consts, 8)
            for j in range(4):
                q = slice(j * D, (j + 1) * D)
                pool.dma_start(nat[q, 0, q], W0).then_inc(loaded, 16)
                pool.dma_start(nat[q, 1, q], W3).then_inc(loaded, 16)
                pool.dma_start(wdiag[q, 1, q], W2).then_inc(loaded, 16)
                pool.dma_start(wnat[q, 0:BASES, :], W1.rearrange("b i o -> i b o")).then_inc(loaded, 16)
                pool.dma_start(wnat[q, BASES, :], wself).then_inc(loaded, 16)
                pool.dma_start(anat[:, 0, j, :], A1).then_inc(loaded, 16)
                pool.dma_start(anat[:, 1, j, :], A2).then_inc(loaded, 16)
            pool.dma_start(bias1[:, 0:D], A1b.partition_broadcast(P)).then_inc(loaded, 16)
            pool.dma_start(bias1[:, D:], A2b.partition_broadcast(P)).then_inc(loaded, 16)
            for k, b in enumerate((b0, b2, b3)):
                pool.dma_start(biasrow[:, k, :], b.rearrange("(a f) -> a f", a=1)).then_inc(loaded, 16)
            pool.dma_start(relc[0:RELS, 0:BASES], wcomp).then_inc(loaded, 16)
            pool.dma_start(relc[0:RELS, BASES:YC], relemb).then_inc(loaded, 16)
            pool.dma_start(opeps[:, :], eps0.partition_broadcast(P)).then_inc(loaded, 16)

            pool.wait_ge(extra_ready, 1)
            pool.wait_ge(rows_out, 32)
            pool.indirect_dma_start(out=xrow[0:EXTRAS].rearrange("p a e -> p (a e)"), out_offset=None, in_=rowsD,
                                    in_offset=bass.IndirectOffsetOnAxis(ap=tcoli[0:EXTRAS, 0:1], axis=0)
                                    ).then_inc(extra_rows, 16)
            halves = edge_attr.rearrange("(r e) f -> r (e f)", e=HALF)
            X = slice(0, EXW)
            for k in range(2):
                pool.indirect_dma_start(out=xattr[X, k * HALF * D:(k + 1) * HALF * D], out_offset=None, in_=halves,
                                        in_offset=bass.IndirectOffsetOnAxis(ap=tcoli[X, 1 + k:2 + k], axis=0)
                                        ).then_inc(extra_attr, 16)

            for l in range(4):
                to = g1 if l == 1 else grow
                written = (table_out[l], BANKS * 16)
                if l == 1:
                    for k in range(LOTS):
                        written = (p1_out[k], 16 * ((P1_LOTS - 1 - k) // LOTS + 1))
                        pool.wait_ge(*written)

                def body(n, self_loop, lots=LOTS):
                    for k in range(lots):
                        pool.wait_ge(written[0], written[1])
                        pool.wait_ge(idx_ready[k], n)
                        pool.wait_ge((row_used, row_used, msg_ready, msg_ready)[l][k], n)
                        for u in range(HB):
                            pool.indirect_dma_start(
                                out=to[:, k, u, :], out_offset=None, in_=tableD[l],
                                in_offset=bass.IndirectOffsetOnAxis(ap=idx[:, k, u:u + 1], axis=0)
                            ).then_inc(gathered[l][k], 16)
                    if self_loop:
                        pool.wait_ge(self_out, BANKS * 16)
                        pool.wait_ge(self_idx_ready, n)
                        pool.wait_ge(self_used, n)
                        pool.indirect_dma_start(
                            out=selfrow[:, :], out_offset=None, in_=selfD,
                            in_offset=bass.IndirectOffsetOnAxis(ap=selfidx[:, 0:1], axis=0)
                        ).then_inc(self_gathered, 16)

                first = BEFORE[l] + 1
                if l == 1:
                    with pool.Fori(first, first + BLOCKS) as n:
                        body(n, True)
                    first += BLOCKS
                with pool.Fori(first, BEFORE[l + 1] + (1 if l == 1 else 0)) as n:
                    body(n, False)
                if l != 1:
                    body(BEFORE[l + 1], False, LAST_LOTS)

        @block.scalar
        def _(act):
            tf, hf, xf = (v[:, :, :].rearrange("p b f -> p (b f)") for v in (t, h, x))

            def columns(b):
                return slice(b * BANK, min((b + 1) * BANK, FEAT))

            def square(l, b):
                act.wait_ge(centered, BANKS * l + b + 1)
                nc.scalar.activation(tf[:, columns(b)], hf[:, columns(b)], ACT.Square).then_inc(squared, 1)

            def norm(l, done):
                for b in range(done, BANKS):
                    square(l, b)
                act.wait_ge(var_ready, l + 1)
                nc.scalar.activation(small[:, 2], small[:, 1], ACT.Sqrt).then_inc(std_ready, 1)

            norm(0, 0)

            act.wait_ge(ends_loaded, 9 * 16)
            nc.scalar.copy(rows[:, :, DST, :], raw[:, 0]).then_inc(rows_cast, 1)
            act.wait_ge(kinds_loaded, 6 * 16)
            nc.scalar.copy(rows[:, :, ETY, :], raw[:, 3]).then_inc(rows_cast, 1)
            nc.scalar.copy(rbf[:, :, 1, :], raw[:, 3]).then_inc(local_ready, 1)

            act.wait_ge(src_T, 1)
            for b in range(-(-ROWCH // 4)):
                at = b * BANK
                n = min(BANK, TILES - at)
                last = nc.scalar.copy(tabs[:, SRC, EXN + at:EXN + at + n], ps[:, at:at + n])
            last.then_inc(src_copied, 1)

            def lot(l, i, k):
                nc.scalar.copy(idx[:, k, :], srcT[:, bass.ds(i * BODY + (FIRST[l] + k * HB), HB)]
                               ).then_inc(idx_ready[k], 1)

            act.wait_ge(tabs_ready, 1)
            for k in range(LOTS):
                lot(0, 0, k)

            for c in range(ROWCH + 1):
                n = P if c < FULL_CH else TILES - FULL_CH * P if c == FULL_CH else EXTRAS
                act.wait_ge(tabs_T, c + 1)
                bank = ps[:, (c % 7) * BANK:(c % 7 + 1) * BANK].rearrange("p (a e) -> p a e", a=4)
                if c <= FULL_CH:
                    at = EXN + c * P
                    last = nc.scalar.copy(tabs[:, 0:SRC, at:at + n], bank[:, 0:SRC, 0:n])
                else:
                    nc.scalar.copy(tabs[:, DLOC, 0:EXN], bank[:, DLOC, EXW:EXTRAS])
                    nc.scalar.copy(tabs[:, BLK, XW:XW + EXW], bank[:, DLOC, 0:EXW])
                    nc.scalar.copy(tabs[:, WGT:, 0:EXN], bank[:, WGT:, EXW:EXTRAS])
                    last = nc.scalar.copy(tabs[:, WGT:, XW:XW + EXW], bank[:, WGT:, 0:EXW])
                last.then_inc(tabs_copied, 1)

            def transposes(q, b):
                w = min(BANK, GROUPS * P - b * BANK)
                rows_ = P if b < BANKS - 1 else 2 * D
                act.wait_ge(hT_done, BANKS * q + b + 1)
                nc.scalar.copy(tT[0:rows_, b * BANK:b * BANK + w], ps[0:rows_, b * BANK:b * BANK + w]
                               ).then_inc(hT_copied, 1)

            def linear(l, q):
                def sums(b):
                    nc.scalar.copy(tf[:, columns(b)], ps[:, columns(b)]).then_inc(t_ready, 1)

                if l:
                    for k in range(LOTS):
                        act.wait_ge(mm_done[k], BEFORE[l + 1] + 1)
                    sums(0)
                    sums(1)
                for b in range(BANKS):
                    transposes(q, b)
                    if l and b + 2 < BANKS:
                        sums(b + 2)
                    if l < 3 and b >= 3:
                        square(l + 1, b - 3)
                if l < 3:
                    norm(l + 1, BANKS - 3)

            def next_lot(l, i, k, end):
                if end and l != 1 and k >= LAST_LOTS:
                    act.wait_ge(idx_ready[k], BEFORE[l + 1])
                    act.wait_ge(gathered[l][k], i * 64)
                else:
                    act.wait_ge(gathered[l][k], i * 64 + 64)
                if not end:
                    lot(l, i + 1, k)
                elif l < 3:
                    lot(l + 1, 0, k)

            def lots(l):
                with act.Fori(0, C[l] - 1) as i:
                    for k in range(LOTS):
                        next_lot(l, i, k, False)
                for k in range(LOTS):
                    next_lot(l, C[l] - 1, k, True)

            act.wait_ge(tabs_ready, 2)
            lots(0)
            linear(0, 0)

            def high(b):
                w = slice(b * BLOCKS_IN, min((b + 1) * BLOCKS_IN, BLOCKS))
                act.wait_ge(h_ready, BANKS + b + 1)
                for at in (0, 3):
                    last = nc.scalar.copy(hparts[:, w, at, :], h[:, w, :])
                last.then_inc(high_ready, 1)

            def middle(b):
                w = slice(b * BLOCKS_IN, min((b + 1) * BLOCKS_IN, BLOCKS))
                act.wait_ge(rest_ready, b + 1)
                for at in (1, 4):
                    last = nc.scalar.copy(hparts[:, w, at, :], t[:, w, :])
                last.then_inc(mid_ready, 1)

            def copy_parts(g):
                n = min(4, BLOCKS - 4 * g)
                act.wait_ge(partsT_done, g + 1)
                nc.scalar.copy(partsT[:, g % 6, 0:n], parts_bank(g)[:, 0:n]).then_inc(partsT_copied, 1)

            for b in range(2):
                high(b)
                middle(b)
            for g in range(AHEAD):
                copy_parts(g)
            for g in range(GROUPS):
                for b in range(4 * g, min(4 * g + 4, BLOCKS)):
                    act.wait_ge(p1_done, b + 1)
                    if b >= 16 and b % 4 == 0:
                        act.wait_ge(p1_out[b // 4 % LOTS], 16 * (b // 16))
                    at = (b % 3) * 2 * BANK
                    nc.scalar.copy(trow[:, b % 16, 0:MSG // 2], ps[:, at:at + MSG // 2]).then_inc(p1_copied, 1)
                if g + AHEAD < GROUPS:
                    copy_parts(g + AHEAD)
                b = g // 4 + 2
                if b < BANKS and g % 4 < 2:
                    (high, middle)[g % 4](b)

            def copy_yc(i, k):
                act.wait_ge(yc_done[k], i + 2)
                act.wait_ge(coef_ready[k // 2], i + 1)
                nc.scalar.copy(yc[:, k], ps7).then_inc(yc_copied, 1)

            def attention(i, p):
                act.wait_ge(score_ready[p], i + 1)
                w = slice(2 * p * HB, (2 * p + 2) * HB)
                nc.scalar.activation(att[:, w], score[:, w], ACT.Tanh, scale=float(D) ** -0.5).then_inc(att_ready[p], 1)

            def selector_distances(i, k):
                act.wait_ge(steps_loaded[k], i * 16 + 16)
                act.wait_ge(sel_ready[(k - 1) % LOTS], i + (1 if k == 0 else 2))
                nc.scalar.activation(off[:, :, :, :], rowb[:, k], ACT.Abs, scale=-1.0, bias=part[:, 0:1]
                                     ).then_inc(off_ready[k], 1)

            def selectors(i, k):
                act.wait_ge(off_ready[k], i + 1)
                act.wait_ge(yc_done[k], i + 1)
                nc.scalar.activation(nodeT[:, k], off[:, :, 0, :], ACT.Relu, scale=-1.0, bias=ones[:, 0:1]
                                     ).then_inc(node_sel_ready[k], 1)
                nc.scalar.activation(relT[:, k], off[:, :, 1, :], ACT.Relu, scale=-1.0, bias=ones[:, 0:1]
                                     ).then_inc(sel_ready[k], 1)

            def self_lot(i):
                nc.scalar.copy(selfidx[:, :], selfi[:, bass.ds(i, 1)]).then_inc(self_idx_ready, 1)

            def self_loop(i):
                act.wait_ge(self_gathered, i * 16 + 16)
                nc.scalar.activation(h[:, bass.ds(i, 1), :], selfrow[:, :].unsqueeze(1), ACT.Identity,
                                     scale=has_edge[:, bass.ds(i, 1)]).then_inc(self_used, 1)
                self_lot(i + 1)

            def body1(i, end):
                for k in range(LOTS):
                    ahead = [after(i, k, n, end) for n in range(5)]
                    if k == 0:
                        next_lot(1, i, 0, end)
                    if k + 1 < LOTS:
                        next_lot(1, i, k + 1, end)
                    for u in range(HB):
                        last = nc.scalar.activation(away[:, u, :], iota[:, :], ACT.Abs, scale=-1.0,
                                                    bias=tabs[:, DLOC, bass.ds(i * BODY + (k * HB + u), 1)])
                    last.then_inc(away_ready[k], 1)
                    if ahead[4]:
                        selector_distances(*ahead[4])
                    act.wait_ge(away_ready[k], i + 1)
                    act.wait_ge(mm_done[k], i + (BEFORE[1] + 1))
                    nc.scalar.activation(onehot[:, k], away[:, :, :], ACT.Relu, scale=-1.0, bias=ones[:, 0:1]
                                         ).then_inc(onehot_ready[k], 1)
                    if ahead[4]:
                        selectors(*ahead[4])
                    if k % 2 == 1 and ahead[1]:
                        attention(ahead[1][0], ahead[1][1] // 2)
                    if ahead[3]:
                        copy_yc(*ahead[3])
                    act.wait_ge(onehot_ready[k], i + 1)

            for k in range(4):
                selector_distances(0, k)
                selectors(0, k)
            for k in range(3):
                copy_yc(0, k)
            attention(0, 0)
            act.wait_ge(self_found, 1)
            self_lot(0)
            with act.Fori(0, BLOCKS) as i:
                body1(i, False)
                self_loop(i)
            with act.Fori(BLOCKS, C[1] - 1) as i:
                body1(i, False)
            body1(C[1] - 1, True)
            norm(2, 0)
            lots(2)
            linear(2, 1)
            lots(3)
            linear(3, 2)

        @block.vector
        def _(dve):
            chain = [0]

            def step(ins):
                chain[0] += 1
                ins.then_inc(dve_chain, 1)
                dve.wait_ge(dve_chain, chain[0])

            tt, ts, cp = nc.vector.tensor_tensor, nc.vector.tensor_scalar, nc.vector.tensor_copy

            nc.vector.memset(nat[:, :, :], 0.0).then_inc(consts, 1)
            nc.vector.memset(wdiag[:, 1, :], 0.0).then_inc(consts, 1)
            nc.vector.memset(relc[:, :], 0.0).then_inc(consts, 1)
            nc.vector.memset(zeros[:, :], 0.0).then_inc(consts, 1)
            nc.vector.memset(ones[:, :], 1.0).then_inc(consts, 1)
            nc.vector.memset(padbf[:, 0:P], FAR).then_inc(consts, 1)
            nc.vector.memset(padbf[:, P:2 * P], 0.0).then_inc(consts, 1)
            nc.vector.memset(tcoli[:, 6:7], 0).then_inc(consts, 1)
            nc.vector.memset(tabs[:, WGT:, XW + EXW:COLS], 0.0)
            nc.vector.memset(tabs[:, BLK, XW + EXW:COLS], FAR)
            nc.vector.memset(tabs[:, DLOC, XW:STEPS_N], FAR)
            free = [s[k] for s in (row_used, msg_ready, mm_done, sel_ready, yc_done) for k in range(LOTS)] + coef_ready + [yc_copied]
            for n, s in enumerate(free):
                nc.vector.memset(msg[:, 0, 0, n:n + 1], 0.0).then_inc(s, 1)
            nc.vector.memset(msg[:, 0, 1, 0:1], 0.0).then_inc(self_idx_ready, BEFORE[1])
            nc.vector.memset(msg[:, 0, 1, 1:2], 0.0).then_inc(self_used, BEFORE[1] + 1)
            dve.wait_ge(pads_set, 6)
            cp(iota[:, :], iota_i[:, :])
            step(cp(part[:, :], part_i[:, :]))
            cp(iotab[:, :], iota_i[:, :])
            nc.vector.tensor_scalar_add(part1[:, :], part[:, :], 1.0)
            ts(thr[:, 0:EXW], iota[:, 0:EXW], 1.0, float(WB * P), ALU.add, ALU.mult)
            step(ts(thr[:, EXW:EXTRAS], iota[:, 0:EXN], 1.0, float(P), ALU.add, ALU.mult))

            tf, hf, xf = (v[:, :, :].rearrange("p b f -> p (b f)") for v in (t, h, x))

            def columns(b):
                return slice(b * BANK, min((b + 1) * BANK, FEAT))

            def norm(l, residual):
                total_, var, std, r, a, b_ = (small[:, k] for k in range(6))
                stt = nc.vector.scalar_tensor_tensor

                def of(b):
                    w = slice(b * BLOCKS_IN, min((b + 1) * BLOCKS_IN, BLOCKS))
                    return w, lambda v: v[:, w].unsqueeze(2).to_broadcast([P, w.stop - w.start, D])

                for turn in range(BANKS + 3):
                    b = turn - 3
                    if b >= 0:
                        w, wide = of(b)
                        dve.wait_ge(squared, BANKS * l + b + 1)
                        last = nc.vector.reduce_sum(var[:, w], t[:, w, :], AX.X)
                    b = turn - 2
                    if 0 <= b < BANKS:
                        w, wide = of(b)
                        dve.wait_ge(mean_ready, BANKS * l + b + 1)
                        stt(h[:, w, :], wide(total_), -1.0 / D, x[:, w, :], ALU.mult, ALU.add).then_inc(centered, 1)
                    b = turn - 1
                    if 0 <= b < BANKS:
                        w, wide = of(b)
                        dve.wait_ge(added, BANKS * l + b + 1)
                        nc.vector.reduce_sum(total_[:, w], x[:, w, :], AX.X).then_inc(mean_ready, 1)
                    if turn < BANKS:
                        residual(turn).then_inc(added, 1)
                step(last)
                ts(var, var, 1.0 / D, EPS, ALU.mult, ALU.add).then_inc(var_ready, 1)
                dve.wait_ge(std_ready, l + 1)
                step(nc.vector.reciprocal(r, std))
                step(tt(a, r, r, ALU.mult))
                step(tt(b_, a, var, ALU.mult))
                step(ts(a, b_, -0.5, 1.5, ALU.mult, ALU.add))
                step(tt(b_, a, r, ALU.mult))
                dve.wait_ge(centered, BANKS * (l + 1))
                for b in range(BANKS):
                    w, wide = of(b)
                    stt(h[:, w, :], h[:, w, :], 0.0, wide(b_), ALU.max, ALU.mult).then_inc(h_ready, 1)

            dve.wait_ge(x_loaded, 32)
            norm(0, lambda b: nc.vector.memset(msg[:, 1, 0, b:b + 1], 0.0))

            dve.wait_ge(rows_cast, 1)
            for c in range(ROWCH):
                last = ts(before[:, c, :], thr[:, :], rows[:, c, DST, P - 1:P], None, ALU.is_gt)
            last.then_inc(before_ready, 1)
            dve.wait_ge(ends_loaded, 9 * 16)
            dI, nI, sI = (raw[:, a] for a in range(3))
            tt(wloc[:, :, :], dI, nI, ALU.not_equal)
            nc.vector.tensor_single_scalar(firstwi[:, 0, :], dI[:, :, 0], 7, ALU.arith_shift_right)
            step(nc.vector.tensor_single_scalar(firstwi[:, 2, :], dI[:, :, 0], 7 + WB.bit_length() - 1,
                                                ALU.arith_shift_right))
            step(nc.vector.tensor_single_scalar(nI, sI, P - 1, ALU.bitwise_and))
            step(nc.vector.tensor_single_scalar(sI, sI, 7, ALU.arith_shift_right))
            step(nc.vector.scalar_tensor_tensor(rloc[:, :, :], nI, float(BLOCKS), sI, ALU.mult, ALU.add))
            nc.vector.scalar_tensor_tensor(rows[:, :, RSRC, :], rloc[:, :, :], 2.0, wloc[:, :, :], ALU.mult, ALU.add
                                           ).then_inc(rows_ready, 1)
            cp(firstw[:, 0, :], firstwi[:, 0, :])
            step(cp(firstw[:, 2, :], firstwi[:, 2, :]))
            dve.wait_ge(count_done, 1)
            X = slice(0, EXTRAS)
            step(cp(tcol[X, 0:1], ps[X, 7 * BANK:7 * BANK + 1]))
            cp(tcoli[X, 0:1], tcol[X, 0:1])
            nc.vector.tensor_single_scalar(tcoli[X, 1:2], tcol[X, 0:1], 2.0, ALU.mult)
            step(ts(tcol[X, 1:2], tcol[X, 0:1], 2.0, 1.0, ALU.mult, ALU.add))
            nc.vector.tensor_single_scalar(tcoli[X, 2:3], tcol[X, 1:2], float(N_EDGES // HALF - 1), ALU.min
                                           ).then_inc(extra_ready, 1)
            ts(tcol[X, 2:3], part[X, :], float(EXW), None, ALU.is_ge)
            ts(tcol[X, 3:4], part[X, :], float(P - P * WB), float(P * (1 - EXW) - P * WB), ALU.mult, ALU.add)
            step(nc.vector.tensor_single_scalar(tcol[X, 4:5], part1[X, :], float(P * WB), ALU.mult))
            step(tt(tcol[X, 3:4], tcol[X, 3:4], tcol[X, 2:3], ALU.mult))
            step(tt(tcol[X, 5:6], tcol[X, 3:4], tcol[X, 4:5], ALU.add))
            nc.vector.tensor_single_scalar(tcoli[X, 5:6], tcol[X, 5:6], float(D) / P, ALU.mult)

            dve.wait_ge(rows_ready, 1)
            for a, blocks, to in ((0, 1, rloc), (2, WB, wloc)):
                nc.vector.tensor_single_scalar(firstw[:, a + 1, :], firstw[:, a, :], float(blocks * P), ALU.mult)
                step(nc.vector.tensor_single_scalar(firstwi[:, a + 1, :], firstw[:, a, :], float(blocks * D), ALU.mult))
                tt(to[:, :, :], rows[:, :, DST, :], firstw[:, a + 1, :].unsqueeze(2).to_broadcast([P, ROWCH, P]),
                   ALU.subtract)
            cp(rbf[:, :, 0, :], rloc[:, :, :]).then_inc(local_ready, 1)
            dve.wait_ge(local_ready, 2)
            dve.wait_ge(src_copied, 1)
            single = nc.vector.tensor_single_scalar
            main = slice(EXN, XW)
            step(cp(tmpi[:, 0, main], tabs[:, SRC, main]))
            single(srcT[:, main], tmpi[:, 0, main], 1, ALU.arith_shift_right).then_inc(tabs_ready, 1)
            dve.wait_ge(loaded, 36 * 16)
            step(nc.vector.tensor_scalar_add(opeps[:, :], opeps[:, :], 1.0))
            cp(wq[:, 0:MSG].rearrange("p (o b) -> p o b", o=D), wnat[:, 0:BASES, :].rearrange("p b o -> p o b"))
            cp(wq[:, MSG + D:MSG + 2 * D], wnat[:, BASES, :])
            of = relc[:, :]
            for k in range(3):
                step(cp(relparts[:, k, :], of))
                if k < 2:
                    step(tt(relrest[:, k, :], of, relparts[:, k, :], ALU.subtract))
                    of = relrest[:, k, :]
            dve.wait_ge(wts_T, 1)
            cp(wdiag[:, 0, :], ps[:, W7:W7 + P])
            cp(wdiag[:, 2, :], ps[:, W7 + P:W7 + 2 * P])
            cp(identb[:, :], ident[:, :])
            cp(wq[:, MSG:MSG + D], ps[:, W7 + 2 * P:W7 + 2 * P + D])
            cp(wq[:, MSG + 2 * D:PROD], ps[:, W7 + 2 * P + D:W7 + 2 * P + 2 * D]).then_inc(wts_ready, 1)

            dve.wait_ge(extra_rows, 16)
            step(tt(tcol[X, 6:7], xrow[X, DST, 0:1], tcol[X, 5:6], ALU.is_ge))
            step(nc.vector.tensor_single_scalar(tcol[X, 6:7], tcol[X, 6:7], FAR, ALU.mult))
            step(tt(tcol[X, 7:8], tcol[X, 6:7], tcol[X, 5:6], ALU.subtract))
            step(ts(xloc[X, :], xrow[X, DST, :], tcol[X, 7:8], None, ALU.add))
            cp(xbf[X, 0, :], xloc[X, :])
            cp(xbf[X, 1, :], xrow[X, ETY, :]).then_inc(xlocal_ready, 1)

            dve.wait_ge(wts_ready, 1)
            step(cp(wsplit[:, 0, :], wq[:, :]))
            step(tt(wrest, wq[:, :], wsplit[:, 0, :], ALU.subtract))
            step(cp(wsplit[:, 1, :], wrest))
            step(tt(wsplit[:, 2, :], wrest, wsplit[:, 1, :], ALU.subtract))
            for k, (_, of) in enumerate(PASSES):
                for j in range(4):
                    q = slice(j * D, (j + 1) * D)
                    last = cp(wparts[q, k, :], wsplit[q, of[j], :])
            step(last)

            dve.wait_ge(tabs_copied, ROWCH + 1)
            extra = (slice(0, EXN), slice(XW, COLS))
            for e in extra:
                last = cp(tmpi[:, 0, e], tabs[:, SRC, e])
            step(last)
            for e in extra:
                last = single(srcT[:, e], tmpi[:, 0, e], 1, ALU.arith_shift_right)
            last.then_inc(tabs_ready, 1)
            step(single(tmpi[:, 1, :], tmpi[:, 0, :], 1, ALU.bitwise_and))
            dve.wait_ge(tabs_ready, 2)
            step(nc.vector.scalar_tensor_tensor(tmpi[:, 0, :], srcT, 1.0, tmpi[:, 1, :], ALU.add, ALU.mult))
            step(single(tmpi[:, 1, :], tmpi[:, 0, :], 7, ALU.arith_shift_right))
            step(cp(lastT[:, 0, :], tmpi[:, 1, :]))
            step(single(tmpi[:, 1, :], tmpi[:, 0, :], P - 1, ALU.bitwise_and))
            step(cp(lastT[:, 1, :], tmpi[:, 1, :]))
            W = slice(EXN, COLS)
            step(cp(tmpi[:, 0, W], tabs[:, BLK, W]))
            step(single(tmpi[:, 1, W], tmpi[:, 0, W], P - 1, ALU.bitwise_and))
            step(cp(node[:, W], tmpi[:, 1, W]))
            step(single(tmpi[:, 1, W], tmpi[:, 0, W], 7, ALU.arith_shift_right))
            step(cp(tabs[:, BLK, W], tmpi[:, 1, W]))

            def masks(l, i, k):
                dve.wait_ge(mm_done[k], i + (BEFORE[l] + 1))
                tt(mask[:, k], iota[:, 0:WB].unsqueeze(1).to_broadcast([P, HB, WB]), per_edge(BLK, i, k), ALU.is_equal
                   ).then_inc(masked[k], 1)

            def onehots(i, k, to):
                tt(to[:, k], iotab[:, :].unsqueeze(1).to_broadcast([P, HB, P]),
                   node[:, bass.ds(i * BODY + (EXN + k * HB), HB)].unsqueeze(2).to_broadcast([P, HB, P]), ALU.is_equal)

            def per_edge(v, i, k):
                return tabs[:, v, bass.ds(i * BODY + (EXN + k * HB), HB)].unsqueeze(2).to_broadcast([P, HB, WB])

            def spread(k, rows_, factors):
                tt(wmsg[:, k], rows_[:, k].unsqueeze(2).to_broadcast([P, HB, WB, D]),
                   factors[:, k].unsqueeze(3).to_broadcast([P, HB, WB, D]), ALU.mult).then_inc(msg_ready[k], 1)

            def wide_layer(l, body):
                with dve.Fori(0, C[l] - 1) as i:
                    body(i, LOTS)
                body(C[l] - 1, LAST_LOTS)
                for n, k in enumerate(range(LAST_LOTS, LOTS)):
                    for m, s in enumerate((masked, msg_ready, mm_done) + ((row_used,) if l == 0 else ())):
                        nc.vector.memset(unused[:, l, n, m:m + 1], 0.0).then_inc(s[k], 1)

            def body0(i, lots_):
                for k in range(lots_):
                    masks(0, i, k)
                    dve.wait_ge(gathered[0][k], i * 64 + 64)
                    dve.wait_ge(attr_loaded[k], i * 16 + 16)
                    tt(total[:, k], grow[:, k], attr[:, k], ALU.add).then_inc(row_used[k], 1)
                    onehots(i, k, onehot)
                    onehots(i, k, onehotb)
                    dve.wait_ge(masked[k], i + 1)
                    for a in range(2):
                        tt(lastrow[:, k, :, a, :], mask[:, k],
                           lastT[:, a, bass.ds(i * BODY + (EXN + k * HB), HB)].unsqueeze(2).to_broadcast([P, HB, WB]),
                           ALU.mult)
                    dve.wait_ge(row_used[k], i + 2)
                    for u in range(HB):
                        last = nc.vector.scalar_tensor_tensor(
                            wmsg[:, k, u], total[:, k, u].unsqueeze(1).to_broadcast([P, WB, D]), 0.0,
                            mask[:, k, u].unsqueeze(2).to_broadcast([P, WB, D]), ALU.max, ALU.mult)
                    last.then_inc(msg_ready[k], 1)

            wide_layer(0, body0)

            def linear_residual(q, relu):
                def add(b):
                    w = columns(b)
                    dve.wait_ge(lin_done, BANKS * q + b + 1)
                    if relu:
                        return nc.vector.scalar_tensor_tensor(xf[:, w], ps[:, w], 0.0, xf[:, w], ALU.max, ALU.add)
                    return tt(xf[:, w], ps[:, w], xf[:, w], ALU.add)
                return add

            def scattered(l):
                for k in range(LOTS):
                    dve.wait_ge(mm_done[k], BEFORE[l + 1] + 1)

            scattered(0)
            parts_ = ps[:, ID0:ID0 + WINW * ID].rearrange("p (w a b) -> p a w b", a=2, b=WB)
            by_window = lambda v: v[:, :].rearrange("p (w b) -> p w b", b=WB)
            step(cp(by_window(selfv), parts_[:, 1]))
            step(nc.vector.scalar_tensor_tensor(by_window(selfv), parts_[:, 0], float(P), by_window(selfv),
                                                ALU.mult, ALU.add))
            nc.vector.tensor_single_scalar(has_edge[:, :], selfv[:, :], 1.0, ALU.min)
            ts(selfi[:, :], selfv[:, :], -1.0, 0.0, ALU.add, ALU.max).then_inc(self_found, 1)
            for b in range(BANKS):
                w = columns(b)
                nc.vector.scalar_tensor_tensor(tf[:, w], hf[:, w], opeps[:, 0:1], acc[:, w], ALU.mult, ALU.add
                                               ).then_inc(t_ready, 1)
            norm(1, linear_residual(0, False))
            yf = y[:, :, :].rearrange("p b f -> p (b f)")

            def rest(b):
                w = slice(b * BLOCKS_IN, min((b + 1) * BLOCKS_IN, BLOCKS))
                dve.wait_ge(high_ready, b + 1)
                tt(r1[:, w, :], h[:, w, :], hparts[:, w, 0, :], ALU.subtract).then_inc(rest_ready, 1)

            def low(b):
                w = slice(b * BLOCKS_IN, min((b + 1) * BLOCKS_IN, BLOCKS))
                dve.wait_ge(mid_ready, b + 1)
                tt(hparts[:, w, 2, :], r1[:, w, :], hparts[:, w, 1, :], ALU.subtract).then_inc(parts_ready, 1)

            r1 = t
            for b in range(2):
                rest(b)
                low(b)
            for g in range(GROUPS):
                for b in range(4 * g, min(4 * g + 4, BLOCKS)):
                    at = (b % 3) * 2 * BANK + BANK
                    dve.wait_ge(p1_done, b + 1)
                    if b >= 16 and b % 4 == 0:
                        dve.wait_ge(p1_out[b // 4 % LOTS], 16 * (b // 16))
                    cp(trow[:, b % 16, MSG // 2:MSG], ps[:, at:at + MSG // 2])
                    at += MSG // 2
                    tt(trow[:, b % 16, MSG:ROW1], ps[:, at:at + D], bias1[:, 0:D], ALU.add)
                    cp(h[:, b, :], ps[:, at + D:at + 2 * D])
                    tt(yf[:, b * D:(b + 1) * D], ps[:, at + 2 * D:at + 3 * D], bias1[:, D:2 * D], ALU.add
                       ).then_inc(p1_biased, 1)
                b = g // 4 + 2
                if b < BANKS and g % 4 < 2:
                    (rest, low)[g % 4](b)

            def score_terms(i, p, first=False):
                for k in (2 * p, 2 * p + 1):
                    dve.wait_ge(gathered[1][k], i * 64 + 64)
                dve.wait_ge(yc_copied, i * LOTS + (2 * p + 3))
                if not first:
                    dve.wait_ge(score_ready[1 - p], i + p)
                tt(yprod[:, :, :], pair(p, g1)[:, :, MSG:ROW1], pair(p, yc)[:, :, BASES:YC], ALU.mult
                   ).then_inc(yprod_ready[p], 1)

            def score_sum(i, p):
                dve.wait_ge(yprod_ready[p], i + 1)
                nc.vector.reduce_sum(score[:, 2 * p * HB:(2 * p + 2) * HB], yprod[:, :, :], AX.X
                                     ).then_inc(score_ready[p], 1)

            def coefficients(i, p):
                dve.wait_ge(att_ready[p], i + 1)
                w = slice(2 * p * HB, (2 * p + 2) * HB)
                nc.vector.scalar_tensor_tensor(pair(p, coef), att[:, w].unsqueeze(2).to_broadcast([P, 2 * HB, BASES]),
                                               0.0, pair(p, yc)[:, :, 0:BASES], ALU.max, ALU.mult
                                               ).then_inc(coef_ready[p], 1)

            def products(i, k):
                dve.wait_ge(msg_ready[(k - 2) % LOTS], i + (BEFORE[1] + (1 if k < 2 else 2)))
                tt(prods[k % 2][:, :, :, :], g1[:, k, :, 0:MSG].rearrange("p u (o b) -> p u o b", o=D),
                   coef[:, k].unsqueeze(2).to_broadcast([P, HB, D, BASES]), ALU.mult).then_inc(row_used[k], 1)

            def messages(i, k):
                dve.wait_ge(row_used[k], i + (BEFORE[1] + 2))
                dve.wait_ge(mm_done[k], i + (BEFORE[1] + 1))
                nc.vector.reduce_sum(msg[:, k], prods[k % 2][:, :, :, :], AX.X).then_inc(msg_ready[k], 1)

            def body1(i, end):
                for k in (0, 2):
                    ahead = after(i, k, 2, end)
                    if ahead:
                        ahead = (ahead[0], ahead[1] // 2)
                    dve.wait_ge(coef_ready[k // 2], i + 2)
                    products(i, k)
                    products(i, k + 1)
                    if ahead:
                        score_terms(*ahead)
                        score_sum(*ahead)
                    messages(i, k)
                    if ahead:
                        coefficients(*ahead)
                    messages(i, k + 1)

            score_terms(0, 0, first=True)
            score_sum(0, 0)
            coefficients(0, 0)
            with dve.Fori(0, C[1] - 1) as i:
                body1(i, False)
            body1(C[1] - 1, True)
            scattered(1)
            dve.wait_ge(self_used, BEFORE[1] + 1 + BLOCKS)

            def add_self(b):
                w = columns(b)
                step(tt(hf[:, w], acc[:, w], hf[:, w], ALU.add))
                return nc.vector.scalar_tensor_tensor(xf[:, w], hf[:, w], 0.0, xf[:, w], ALU.max, ALU.add)

            norm(2, add_self)

            def body2(i, lots_):
                for k in range(lots_):
                    masks(2, i, k)
                    onehots(i, k, onehot)
                    dve.wait_ge(masked[k], i + (C[0] + 1))
                    tt(wmask[:, k], mask[:, k], per_edge(WGT, i, k), ALU.mult).then_inc(weighted[k], 1)
                    dve.wait_ge(gathered[2][k], i * 64 + 64)
                    dve.wait_ge(weighted[k], i + 1)
                    spread(k, grow, wmask)

            wide_layer(2, body2)
            norm(3, linear_residual(1, True))

            def body3(i, lots_):
                for k in range(lots_):
                    masks(3, i, k)
                    onehots(i, k, onehot)
                    dve.wait_ge(gathered[3][k], i * 64 + 64)
                    dve.wait_ge(masked[k], i + (C[0] + C[2] + 1))
                    spread(k, grow, mask)

            wide_layer(3, body3)
            last_add = linear_residual(2, False)
            for b in range(BANKS):
                last_add(b).then_inc(added, 1)

        @block.tensor
        def _(pe):
            mm = nc.tensor.matmul
            pe.wait_ge(consts, 8)
            pe.wait_ge(ident_ready, 2)
            pe.wait_ge(before_ready, 1)
            for c in range(ROWCH):
                last = mm(ps[0:EXTRAS, 7 * BANK:7 * BANK + 1], before[:, c, :], ones[:, 0:1], start=(c == 0),
                          stop=(c == ROWCH - 1))
            last.then_inc(count_done, 1)
            pe.wait_ge(rows_ready, 1)
            for c in range(ROWCH):
                n = P if c < FULL_CH else TILES - FULL_CH * P
                last = nc.tensor.transpose(ps[:, c * P:c * P + n], rows[0:n, c, RSRC, :], ident[0:n, 0:n])
            last.then_inc(src_T, 1)
            pe.wait_ge(extra_ready, 1)
            pe.wait_ge(loaded, 36 * 16)
            nc.tensor.transpose(ps[:, W7:W7 + P], nat[:, 0, :], ident[:, :])
            nc.tensor.transpose(ps[:, W7 + P:W7 + 2 * P], nat[:, 1, :], ident[:, :])
            nc.tensor.transpose(ps[:, W7 + 2 * P:W7 + 2 * P + D], anat[:, 0].rearrange("o r i -> o (r i)"), ident[0:D, 0:D])
            nc.tensor.transpose(ps[:, W7 + 2 * P + D:W7 + 2 * P + 2 * D], anat[:, 1].rearrange("o r i -> o (r i)"),
                                ident[0:D, 0:D]).then_inc(wts_T, 1)

            pe.wait_ge(src_copied, 1)
            pe.wait_ge(local_ready, 2)
            pe.wait_ge(kinds_loaded, 6 * 16)
            for c in range(ROWCH + 1):
                n = P if c < FULL_CH else TILES - FULL_CH * P if c == FULL_CH else EXTRAS
                if c > FULL_CH:
                    pe.wait_ge(xlocal_ready, 1)
                if c >= 7:
                    pe.wait_ge(tabs_copied, c - 6)
                if c > FULL_CH:
                    of = ((DLOC, xloc[0:n, :]), (WGT, xrow[0:n, RWGT, :]), (SRC, xrow[0:n, RSRC, :]))
                else:
                    of = ((DLOC, rloc[0:n, c, :]), (BLK, wloc[0:n, c, :]), (WGT, rows[0:n, c, RWGT, :]))
                for a, v in of:
                    at = (c % 7) * BANK + a * P
                    last = nc.tensor.transpose(ps[:, at:at + n], v, ident[0:n, 0:n])
                last.then_inc(tabs_T, 1)
            pe.wait_ge(tabs_copied, ROWCH + 1)
            pe.wait_ge(wts_ready, 1)
            pe.wait_ge(window_loaded, 16)

            def clear():
                for b in range(BANKS):
                    mm(ps[:, b * BANK:(b + 1) * BANK], zeros[0:1, 0:P], zeros[0:1, :], start=True, stop=True,
                       skip_group_check=True)

            def windows(i, n):
                _, w = nc.values_load_multi_w_load_instructions(
                    window[0:1, bass.ds(i * BODY, n)], engines=(mybir.EngineType.PE,), min_val=0,
                    max_val=(BLOCKS - 1) * D, skip_runtime_bounds_check_because="windows of nodes below N_NODES")
                return w

            def scatter(l, i, k, w, of):
                pe.wait_ge(msg_ready[k], i + (BEFORE[l] + 2))
                for u in range(HB):
                    rhs = of[:, k, u] if l == 1 else of[:, k, u].rearrange("p w f -> p (w f)")
                    last = mm(ps[:, bass.ds(w[u], rhs.shape[-1])], onehot[:, k, u, :], rhs, start=False, stop=True,
                              skip_group_check=True)
                    if l == 0:
                        last = mm(ps[:, bass.ds((w[u] >> (WB * D // ID).bit_length() - 1) + ID0, ID)],
                                  onehotb[:, k, u, :], lastrow[:, k, u].rearrange("p a b -> p (a b)"),
                                  start=False, stop=True, skip_group_check=True)
                last.then_inc(mm_done[k], 1)

            def scatters(l):
                with pe.Fori(0, C[l] - 1) as i:
                    w = windows(i, BODY)
                    for k in range(LOTS):
                        scatter(l, i, k, w[k * HB:], wmsg)
                w = windows(C[l] - 1, LAST_LOTS * HB)
                for k in range(LAST_LOTS):
                    scatter(l, C[l] - 1, k, w[k * HB:], wmsg)

            def transposes(of, b):
                for g in range(4 * b, min(4 * b + 4, GROUPS)):
                    n = min(P, FEAT - g * P)
                    last = nc.tensor.transpose(ps[0:n, g * P:(g + 1) * P], of[:, g * P:g * P + n], ident[:, :])
                last.then_inc(hT_done, 1)

            tf, hf = (v[:, :, :].rearrange("p b f -> p (b f)") for v in (t, h))

            def linear(q, w, bias):
                for turn in range(BANKS + 1):
                    if turn < BANKS:
                        pe.wait_ge(t_ready, BANKS * q + turn + 1)
                        transposes(tf, turn)
                    b = turn - 1
                    if b < 0:
                        continue
                    n = min(BANK, FEAT - b * BANK)
                    pe.wait_ge(hT_copied, BANKS * q + b + 1)
                    mm(ps[:, b * BANK:b * BANK + n], ones[0:1, :], biasrow[:, bias, :].unsqueeze(1).to_broadcast([1, n // D, D]), start=True, stop=False,
                       skip_group_check=True)
                    for g in range(4 * b, min(4 * b + 4, GROUPS)):
                        m = min(P, FEAT - g * P)
                        last = mm(ps[:, g * P:g * P + m], tT[0:m, g * P:(g + 1) * P], wdiag[0:m, w, 0:m],
                                  start=False, stop=True, skip_group_check=True)
                    last.then_inc(lin_done, 1)

            clear()
            scatters(0)
            linear(0, 0, 0)

            def transpose_parts(g):
                four = range(4 * g, min(4 * g + 4, BLOCKS))
                pe.wait_ge(parts_ready, four[-1] // BLOCKS_IN + 1)
                for b in four:
                    for k, (first, _) in enumerate(PASSES):
                        last = nc.tensor.transpose(parts_bank(g)[:, b % 4, k, :],
                                                   hparts[:, b, first:first + 4, :].rearrange("p a f -> p (a f)"),
                                                   identb[:, :])
                last.then_inc(partsT_done, 1)

            for g in range(AHEAD):
                transpose_parts(g)
            for g in range(GROUPS):
                pe.wait_ge(partsT_copied, g + 1)
                for b in range(4 * g, min(4 * g + 4, BLOCKS)):
                    if b >= 3:
                        pe.wait_ge(p1_copied, b - 2)
                        pe.wait_ge(p1_biased, b - 2)
                    at = (b % 3) * 2 * BANK
                    for k in range(2):
                        lhsT = partsT[:, g % 6, b % 4, k, :]
                        mm(ps[:, at:at + MSG // 2], lhsT, wparts[:, k, 0:MSG // 2], start=(k == 0), stop=(k == 1))
                        last = mm(ps[:, at + BANK:at + BANK + PROD - MSG // 2], lhsT, wparts[:, k, MSG // 2:],
                                  start=(k == 0), stop=(k == 1))
                    last.then_inc(p1_done, 1)
                if g + AHEAD < GROUPS:
                    transpose_parts(g + AHEAD)
            pe.wait_ge(p1_copied, BLOCKS)
            pe.wait_ge(p1_biased, BLOCKS)
            clear()

            def edge_terms(i, k, w, n):
                pe.wait_ge(node_sel_ready[k], i + 1)
                pe.wait_ge(sel_ready[k], i + 2)
                pe.wait_ge(yc_copied, n)
                for u in range(HB):
                    for part_ in range(3):
                        mm(ps7[:, u, :], relT[:, k, u, :], relparts[:, part_, :], start=(part_ == 0), stop=False,
                           skip_group_check=True)
                    last = mm(ps7[:, u, BASES:YC], nodeT[:, k, u, :], yf[:, bass.ds(w[u], D)], start=False, stop=True,
                              skip_group_check=True)
                last.then_inc(yc_done[k], 1)

            yf = tf
            def body1(i, end):
                w = windows(i, BODY if end else BODY + LOTS * HB)
                for k in range(LOTS):
                    if after(i, k, LOTS, end):
                        edge_terms(*after(i, k, LOTS, end), w[(k + LOTS) * HB:], i * LOTS + (k + LOTS + 1))
                    pe.wait_ge(onehot_ready[k], i + 1)
                    scatter(1, i, k, w[k * HB:], msg)

            pe.wait_ge(window_loaded, 32)
            w = windows(0, LOTS * HB)
            for k in range(LOTS):
                edge_terms(0, k, w[k * HB:], k + 1)
            with pe.Fori(0, C[1] - 1) as i:
                body1(i, False)
            body1(C[1] - 1, True)
            pe.wait_ge(added, 3 * BANKS)
            clear()
            pe.wait_ge(window_loaded, 48)
            scatters(2)
            linear(1, 1, 1)
            pe.wait_ge(added, 4 * BANKS)
            clear()
            scatters(3)
            linear(2, 2, 2)


_INS = ['x', 'src', 'dst', 'edge_attr_32', 'edge_type_86', 'edge_weight', 'L0_gnn_W', 'L0_gnn_b', 'L0_gnn_eps',
        'L1_gnn_weight', 'L1_gnn_w_comp', 'L1_gnn_self_loop_weight', 'L1_gnn_A1_w', 'L1_gnn_A1_b', 'L1_gnn_A2_w',
        'L1_gnn_A2_b', 'L1_gnn_rel_emb', 'L2_gnn_W', 'L2_gnn_b', 'L3_gnn_W', 'L3_gnn_b']


def kernel(**inputs):
    import numpy as _np
    import concourse.bacc as _bacc
    from concourse import mybir as _mybir
    from concourse.bass_utils import run_bass_kernel_spmd as _run

    nc = _bacc.Bacc("TRN2", target_bir_lowering=False, num_devices=1)
    arrays, args = {}, []
    for name in _INS:
        a = _np.ascontiguousarray(inputs[name])
        arrays[f"in_{name}"] = a
        args.append(nc.dram_tensor(f"in_{name}", a.shape, _mybir.dt.from_np(a.dtype), kind="ExternalInput").ap())
    out = nc.dram_tensor("out_nodes", (N_NODES, D), F32, kind="ExternalOutput").ap()
    gnn(nc, *args, out)
    r = _run(nc, [arrays], core_ids=[0])
    return r.results[0]["out_nodes"]
```
